# Optimizing a Trainium2 kernel written in Bass

```python
import numpy as np
import jax
import jax.numpy as jnp

def _softmax(x, axis=-1):
    return jax.nn.softmax(x, axis=axis)

def _gelu(x):
    return jax.nn.gelu(x, approximate=True)

def _silu(x):
    return jax.nn.silu(x)

def _sigmoid(x):
    return jax.nn.sigmoid(x)

def _layernorm(x, axis=-1, eps=1e-05):
    m = jnp.mean(x, axis=axis, keepdims=True)
    v = jnp.var(x, axis=axis, keepdims=True)
    return (x - m) / jnp.sqrt(v + eps)

def _scatter_add(tgt, idx, src, axis=0):
    return tgt.at[idx].add(src)

def _segment_sum(src, seg, n):
    return jax.ops.segment_sum(src, seg, n)
kernel_name = 'mk_adj_preln_d2_adj_r2_c40eba'

def setup_inputs(seed: int=0):
    np.random.seed(seed)
    _w = jnp.asarray

    def _rec_inputs():
        import jax
        import jax.numpy as jnp
        _gk = jax.random.key(seed)
        x = -0.0002037 + 1 * jax.random.normal(jax.random.fold_in(_gk, 1), (5000, 128), jnp.float32)
        _a = jax.random.bernoulli(jax.random.fold_in(_gk, 2), 0.0032, (5000, 5000))
        _af = _a.astype(jnp.float32)
        adj = _af
        return (x, adj)
    x, adj = _rec_inputs()

    def _L0_gnn_setup():
        import jax, jax.numpy as jnp
        import numpy as np
        N = 5000
        F = 128
        C = 16
        AL = 0.1
        EPS = 1e-12
        key = jax.random.key(seed)
        k1, k2, k3, k4 = jax.random.split(key, 4)
        A = (jax.random.uniform(k1, (N, N)) > 0.99).astype(jnp.float32)
        x = jax.random.normal(k2, (N, F), dtype=jnp.float32)
        h0 = jax.random.normal(k3, (N, F), dtype=jnp.float32)
        labels = jax.random.randint(k4, (N,), 0, C)
        y = jax.nn.one_hot(labels, C, dtype=jnp.float32)
        return {'input': x, 'A': A, 'h0': h0, 'y': y}
    _L0_gnn_all = _L0_gnn_setup()
    _L0_gnn_in = {k: v for k, v in _L0_gnn_all.items() if k in ('h0', 'y')}
    del _L0_gnn_all

    def _L1_gnn_setup():
        import jax, jax.numpy as jnp
        import numpy as np
        N = 4096
        D = 128
        ALPHA = 0.2
        NEG_INF = -9000000000000000.0
        key = jax.random.key(seed)
        k1, k2, k3, k4, k5, k6 = jax.random.split(key, 6)
        inputs = jax.random.normal(k1, (N, D), dtype=jnp.float32)
        adj = (jax.random.uniform(k2, (N, N)) < 32.0 / N).astype(jnp.float32)
        adj = jnp.maximum(adj, jnp.eye(N, dtype=jnp.float32))
        cmt_weight = jax.random.uniform(k3, (N, 1), dtype=jnp.float32)
        W = jax.random.normal(k4, (D, D), dtype=jnp.float32) * (1.0 / np.sqrt(D))
        a1 = jax.random.normal(k5, (D, 1), dtype=jnp.float32) * 0.1
        a2 = jax.random.normal(k6, (D, 1), dtype=jnp.float32) * 0.1
        return {'inputs': inputs, 'adj': adj, 'cmt_weight': cmt_weight, 'W': W, 'a1': a1, 'a2': a2}
    _L1_gnn_all = _L1_gnn_setup()
    _L1_gnn_in = {k: v for k, v in _L1_gnn_all.items() if k in ('cmt_weight', 'W', 'a1', 'a2')}
    del _L1_gnn_all
    return {'x': x, 'adj': adj, 'L0_gnn_h0': _L0_gnn_in['h0'], 'L0_gnn_y': _L0_gnn_in['y'], 'L1_gnn_cmt_weight': _L1_gnn_in['cmt_weight'], 'L1_gnn_W': _L1_gnn_in['W'], 'L1_gnn_a1': _L1_gnn_in['a1'], 'L1_gnn_a2': _L1_gnn_in['a2']}

def reference(x, adj, L0_gnn_h0, L0_gnn_y, L1_gnn_cmt_weight, L1_gnn_W, L1_gnn_a1, L1_gnn_a2):
    import jax
    import jax.numpy as jnp

    def _L0_gnn_ref(input, A, h0, y):
        import jax, jax.numpy as jnp
        import numpy as np
        N = 5000
        F = 128
        C = 16
        AL = 0.1
        EPS = 1e-12
        adj = A * (y @ y.T)
        row_l1 = jnp.maximum(jnp.sum(jnp.abs(adj), axis=1, keepdims=True), EPS)
        adj = adj / row_l1
        support = adj @ input
        return (1.0 - AL) * support + AL * h0

    def _L1_gnn_ref(inputs, adj, cmt_weight, W, a1, a2):
        import jax, jax.numpy as jnp
        import numpy as np
        N = 4096
        D = 128
        ALPHA = 0.2
        NEG_INF = -9000000000000000.0
        Wh = inputs @ W
        f1 = Wh @ a1
        f2 = Wh @ a2
        e = jax.nn.leaky_relu(f1 + f2.T, negative_slope=ALPHA)
        scores = jnp.where(adj > 0, e, NEG_INF)
        att = jax.nn.softmax(scores, axis=-1)
        node_out = jax.nn.relu(att @ Wh)
        return node_out
    h = jnp.maximum(_layernorm(x, axis=-1), 0.0)
    x = x + _L0_gnn_ref(h, adj, L0_gnn_h0, L0_gnn_y)
    h = jnp.maximum(_layernorm(x, axis=-1), 0.0)
    x = x + _L1_gnn_ref(h, adj, L1_gnn_cmt_weight, L1_gnn_W, L1_gnn_a1, L1_gnn_a2)
    return x

_drawn_inputs = setup_inputs


def setup_inputs(seed=0):
    import zlib

    import numpy as np

    out = dict(_drawn_inputs(seed))
    spreads = {}
    factors = {'L1_gnn_a1': 3.676}
    for name, (base, spread) in spreads.items():
        noise = np.random.default_rng([zlib.crc32(name.encode()), seed]).standard_normal(out[name].shape)
        drawn = base * np.exp(spread * noise) if base else spread * noise
        out[name] = jnp.asarray(drawn.astype(out[name].dtype))
    for name, factor in factors.items():
        out[name] = (out[name] * factor).astype(out[name].dtype)
    return out
```

```python
from contextlib import ExitStack

import concourse.bass as bass
from concourse import mybir

ALU = mybir.AluOpType
ACT = mybir.ActivationFunctionType
F32 = mybir.dt.float32
F16 = mybir.dt.float16
BF16 = mybir.dt.bfloat16
U8 = mybir.dt.uint8
AX = mybir.AxisListType
RMAX = bass.bass_isa.ReduceOp.max

P = 128
N = 5000
F = 128
C = 16
GROUPS = 10
GR = N // GROUPS
T = 4
ST = (GR - P) // (T - 1)
DUP = P - ST
NT = GROUPS * T
GW = T * P
HALF = GROUPS // 2
PIECES = 10
PW = N // PIECES
SLOTS = 5
EPS = 1e-5
L1_EPS = 1e-12
H_SCALE = 1024.0
B_SCALE = 16384.0
SLOPE = 0.2
MIX = 0.9
PAIRS = NT // 2


def graph_layers(nc, x, adj, h0, y, w, a1, a2, out, spill):
    with ExitStack() as ctx:
        def sb(name, shape, dt=F32):
            return ctx.enter_context(nc.sbuf_tensor(name, shape, dt))

        def sem(name):
            return ctx.enter_context(nc.semaphore(name))

        mask = sb("mask", [P, HALF, NT, GW], U8)
        xs = sb("xs", [P, NT, F])
        stage = sb("stage", [P, T, 2, F + 1])
        ident = sb("ident", [P, P])
        ones = sb("ones", [P, P])
        wx = sb("wx", [P, F + 2])
        wa1 = sb("wa1", [P, P])
        mv = sb("mv", [P, NT, 2])
        inv = sb("inv", [P, NT])
        tmp = sb("tmp", [P, NT])
        const = sb("const", [P, 8])
        rec = sb("rec", [P, T])
        den = sb("den", [P, 2, T])
        arena = sb("arena", [P, 20280])

        def at(lo, n, dt=F32):
            v = arena[:, lo:lo + n]
            return v if dt == F32 else v.bitcast(dt)

        hm = at(0, 5160, F16).rearrange("p (k h c) -> p k h c", k=NT, h=2)
        yt = at(5160, 2560, F16)
        abuf = at(7720, 10000).rearrange("p (s t c) -> p s t c", s=SLOTS, t=T)
        gbuf = at(17720, 1024, F16).rearrange("p (s c) -> p s c", s=4)
        za = at(18744, 1024).rearrange("p (s t c) -> p s t c", s=2, t=T)
        h0buf = at(19768, 512).rearrange("p (t c) -> p t c", t=T)
        ystage = at(7720, NT * C).rearrange("p (k c) -> p k c", k=NT)
        wraw = at(8400, F)
        wT = at(8600, F)
        araw = at(8800, 2)
        stats = at(19768, NT * 6).rearrange("p (k c) -> p k c", k=NT)
        xm = at(0, 10320, F16).rearrange("p (k m h c) -> p k m h c", k=NT, m=2, h=2)
        wh = at(0, 10320).rearrange("p (k c) -> p k c", k=NT)[:, :, F + 1:2 * (F + 1)]
        f1b = at(10320, 5120)
        vbuf = at(15440, 1024, BF16).rearrange("p (s j c) -> p s j c", s=2, j=2)
        mpos = at(16464, 1024, BF16).rearrange("p (s j c) -> p s j c", s=2, j=2)
        mneg = at(17488, 1024, BF16).rearrange("p (s j c) -> p s j c", s=2, j=2)
        hT = at(15440, 1024).rearrange("p (s c) -> p s c", s=2)
        zb = at(17488, 1024).rearrange("p (s t c) -> p s t c", s=2, t=T)
        zx = at(16464, 2064).rearrange("p (s t m c) -> p s t m c", s=2, m=2, t=T)
        cols = at(18544, 1736)

        def col(i, n=NT):
            return cols[:, i * NT:i * NT + n]
        f1c, f2c, nf2, bcol, dcol = col(0), col(1), col(2), col(3), col(4)
        bsc, dsc, bwc, dwc = col(5), col(6), col(7), col(8)
        sc, ac, cc = col(9), col(10), col(11)
        mw = cols[:, 480:480 + F]
        hsum = cols[:, 620:620 + 2 * GROUPS]
        hsb = cols[:, 640:640 + P]
        pm = cols[:, 780:782]
        gm = cols[:, 784:786]
        sm = cols[:, 790:798]
        hs1 = cols[:, 800:801]

        def bank(name):
            return ctx.enter_context(nc.psum_tensor(name, [P, 512], F32))
        bT = [bank("bT0"), bank("bT1")]
        bY = [bank("bY0"), bank("bY1")]
        acc = ctx.enter_context(nc.psum_tensor("acc", [P, 4, 512], F32))
        acc_a = acc[:, 0:2, 0:2 * (F + 1)]
        acc_b = acc[:, :, 0:2 * (F + 1)]
        f1p = bY[0]

        x_in, y_in, w_in = sem("x_in"), sem("y_in"), sem("w_in")
        const_set, ident_set, ones_set = sem("const_set"), sem("ident_set"), sem("ones_set")
        dve_step, pool_step = sem("dve_step"), sem("pool_step")
        yt_raw, yt_set = sem("yt_raw"), sem("yt_set")
        wT_raw, wT_set, wa_raw, wx_set = sem("wT_raw"), sem("wT_set"), sem("wa_raw"), sem("wx_set")
        var_set, std_set = sem("var_set"), sem("std_set")
        za_set, za_split, h_set = sem("za_set"), sem("za_split"), sem("h_set")
        adj_in = [sem(f"adj_in{i}") for i in range(SLOTS)]
        blk_t, blk_y = sem("blk_t"), sem("blk_y")
        mask_set, g_set, g_used = sem("mask_set"), sem("g_set"), sem("g_used")
        staged_a, rec_a, stage_free = sem("staged_a"), sem("rec_a"), sem("stage_free")
        h0_in, x1_set, spilled, slot_free = sem("h0_in"), sem("x1_set"), sem("spilled"), sem("slot_free")
        var2_set, std2_set = sem("var2_set"), sem("std2_set")
        zb_set, ht_raw, ht_set = sem("zb_set"), sem("ht_raw"), sem("ht_set")
        wh_raw, wh_out, f1_raw, f1_out = sem("wh_raw"), sem("wh_out"), sem("f1_raw"), sem("f1_out")
        hs_set, hsb_set, mean_raw, mw_set = sem("hs_set"), sem("hsb_set"), sem("mean_raw"), sem("mw_set")
        pm_set, gm_set, sm_set, bd_set = sem("pm_set"), sem("gm_set"), sem("sm_set"), sem("bd_set")
        row_set, ac_set = sem("row_set"), sem("ac_set")
        zx_set, zx_hi, xm_set = sem("zx_set"), sem("zx_hi"), sem("xm_set")
        reloaded, f1p_set, v_set = sem("reloaded"), sem("f1p_set"), sem("v_set")
        mp_set, mn_set, m_used = sem("mp_set"), sem("mn_set"), sem("m_used")
        staged_b, num_b, rec_b, stageb_free = sem("staged_b"), sem("num_b"), sem("rec_b"), sem("stageb_free")
        out_ready, out_done, relu_turn = sem("out_ready"), sem("out_done"), sem("relu_turn")

        def rows(src, row0, width, col0=0, ncols=None):
            v = src[bass.ds(row0, GR), :] if not isinstance(row0, int) else src[row0:row0 + GR, :]
            return bass.AP(tensor=v.tensor, offset=v.offset + col0,
                           ap=[[width, P], [ST * width, T], [1, ncols or width]])


        def of_turn(q):
            return (q + HALF) % GROUPS

        def ds1(i):
            return slice(i, i + 1) if isinstance(i, int) else bass.ds(i, 1)

        def dsn(i, n):
            return slice(i, i + n) if isinstance(i, int) else bass.ds(i, n)

        block = ctx.enter_context(nc.Block())

        @block.sync
        def _(sp):
            sp.dma_start(wraw, w).then_inc(w_in, 16)
            sp.dma_start(araw[:, 0:1], a1).then_inc(w_in, 16)
            sp.dma_start(araw[:, 1:2], a2).then_inc(w_in, 16)
            for g in range(GROUPS):
                sp.dma_start(xs[:, g * T:(g + 1) * T, :], rows(x, g * GR, F)).then_inc(x_in, 16)
            for g in range(GROUPS):
                sp.dma_start(ystage[:, g * T:(g + 1) * T, :], rows(y, g * GR, C)).then_inc(y_in, 16)
            sp.wait_ge(yt_raw, GROUPS)
            sp.wait_ge(wa_raw, 1)

            def load(g, i):
                sp.dma_start(abuf[:, i % SLOTS], rows(adj, g * GR, N, i * PW, PW)
                             ).then_inc(adj_in[i % SLOTS], 16)

            for i in range(SLOTS):
                load(0, i)
            with sp.Fori(0, GROUPS - 1) as g:
                for i in range(PIECES):
                    sp.wait_ge(blk_t, g * NT + (i + 1) * T)
                    load(g if i + SLOTS < PIECES else g + 1, (i + SLOTS) % PIECES)
            for i in range(SLOTS):
                sp.wait_ge(blk_t, (GROUPS - 1) * NT + (i + 1) * T)
                load(GROUPS - 1, i + SLOTS)
            for s in range(HALF):
                sp.wait_ge(v_set, (s + 1) * PAIRS)
                sp.dma_start(mask[:, s].rearrange("p k c -> p (k c)"), spill[s]).then_inc(reloaded, 16)
                sp.wait_ge(reloaded, (s + 1) * 16)

        @block.gpsimd
        def _(pool):
            nc.gpsimd.memset(ones[:], 1.0).then_inc(ones_set, 1)
            nc.gpsimd.memset(const[:, 0:1], EPS).then_inc(const_set, 1)
            nc.gpsimd.memset(const[:, 1:2], -2.0).then_inc(const_set, 1)
            nc.gpsimd.memset(const[:, 2:3], 1.0 - MIX).then_inc(pool_step, 1)
            nc.gpsimd.memset(ident[:], 0.0).then_inc(pool_step, 1)
            pool.wait_ge(pool_step, 2)
            nc.gpsimd.affine_select(out=ident[:], in_=ident[:], compare_op=ALU.not_equal, fill=1.0,
                                    base=0, pattern=[[-1, P]], channel_multiplier=1).then_inc(ident_set, 1)
            nc.gpsimd.memset(stage[:], 1.0).then_inc(staged_a, 1)
            pool.sem_inc(slot_free, HALF)
            pool.sem_inc(x1_set, 1)
            stg = stage[:].rearrange("p t m c -> p (t m c)")[:, 0:T * (F + 1)].rearrange(
                "p (t c) -> p t c", t=T)
            pool.wait_ge(var_set, 1)

            def update_a(g, s, spills):
                pool.dma_start(h0buf, rows(h0, g * GR, F)).then_inc(h0_in, 16)
                if spills:
                    pool.wait_ge(mask_set, g * NT + NT)
                    pool.dma_start(spill[bass.ds(s, 1)].rearrange("s p c -> (s p) c"),
                                   mask[:, bass.ds(s, 1)].rearrange("p s k c -> p (s k c)")
                                   ).then_inc(spilled, 16)
                    pool.wait_ge(spilled, s * 16 + 16)
                    pool.sem_inc(slot_free, 1)
                pool.wait_ge(h0_in, g * 16 + 16)
                nc.gpsimd.tensor_tensor(h0buf, h0buf, const[:, 2:3].unsqueeze(2).to_broadcast([P, T, F]),
                                        ALU.mult).then_inc(pool_step, 1)
                pool.wait_ge(rec_a, g + 2)
                nc.gpsimd.tensor_tensor(stg[:, :, 0:F], stg[:, :, 0:F],
                                        rec[:].unsqueeze(2).to_broadcast([P, T, F]), ALU.mult
                                        ).then_inc(pool_step, 1)
                pool.wait_ge(pool_step, g * 3 + 4)
                nc.gpsimd.tensor_tensor(stg[:, :, 0:F], stg[:, :, 0:F], h0buf, ALU.add
                                        ).then_inc(pool_step, 1)
                pool.wait_ge(pool_step, g * 3 + 5)
                xg = xs[:, bass.ds(g * T, T), :]
                nc.gpsimd.tensor_tensor(xg, xg, stg[:, :, 0:F], ALU.add).then_inc(x1_set, 1)
                pool.wait_ge(x1_set, g + 2)

            with pool.Fori(0, HALF) as s:
                update_a(s, s, True)
            with pool.Fori(0, HALF) as s:
                update_a(s + HALF, s, False)
            pool.wait_ge(pm_set, 2)
            nc.gpsimd.partition_all_reduce(gm, pm, P, RMAX).then_inc(gm_set, 1)
            nc.gpsimd.memset(stage[:], 1.0).then_inc(num_b, 1)
            pool.wait_ge(num_b, 1)
            pool.sem_inc(stageb_free, 1)
            pool.sem_inc(staged_b, 1)
            pool.wait_ge(ac_set, 2)
            pool.wait_ge(mw_set, 1)
            done = 2 + 3 * GROUPS
            with pool.Fori(0, GROUPS) as q:
                pool.wait_ge(staged_b, q + 2)
                g4 = of_turn(q) * T
                for m, colv in enumerate((ac, cc)):
                    nc.gpsimd.tensor_tensor(
                        stage[:, :, m, :], stage[:, :, m, :],
                        colv[:, bass.ds(g4, T)].unsqueeze(2).to_broadcast([P, T, F + 1]),
                        ALU.mult).then_inc(pool_step, 1)
                pool.wait_ge(pool_step, q * 6 + (done + 2))
                nc.gpsimd.tensor_tensor(stage[:, :, 0, :], stage[:, :, 0, :], stage[:, :, 1, :],
                                        ALU.add).then_inc(num_b, 1)
                pool.wait_ge(rec_b, q + 2)
                nc.gpsimd.tensor_tensor(stage[:, :, 1, 0:F], mw.unsqueeze(1).to_broadcast([P, T, F]),
                                        den[:, 0, :].unsqueeze(2).to_broadcast([P, T, F]), ALU.mult
                                        ).then_inc(pool_step, 1)
                pool.wait_ge(pool_step, q * 6 + (done + 3))
                nc.gpsimd.tensor_tensor(stage[:, :, 0, 0:F], stage[:, :, 0, 0:F],
                                        stage[:, :, 1, 0:F], ALU.add).then_inc(pool_step, 1)
                pool.wait_ge(pool_step, q * 6 + (done + 4))
                nc.gpsimd.tensor_tensor(stage[:, :, 0, 0:F], stage[:, :, 0, 0:F],
                                        rec[:].unsqueeze(2).to_broadcast([P, T, F]), ALU.mult
                                        ).then_inc(pool_step, 1)
                pool.wait_ge(pool_step, q * 6 + (done + 5))
                pool.sem_inc(relu_turn, 1)
                nc.gpsimd.tensor_scalar(stage[:, :, 0, 0:F], stage[:, :, 0, 0:F], 0.0, None, ALU.max
                                        ).then_inc(pool_step, 1)
                pool.wait_ge(pool_step, q * 6 + (done + 6))
                xg = xs[:, bass.ds(g4, T), :]
                nc.gpsimd.tensor_tensor(xg, xg, stage[:, :, 0, 0:F], ALU.add).then_inc(out_ready, 1)
                pool.wait_ge(out_ready, q + 1)
                pool.sem_inc(stageb_free, 1)
                o = out[bass.ds(of_turn(q) * GR, GR), :]
                pool.dma_start(bass.AP(tensor=o.tensor, offset=o.offset, ap=[[F, ST], [ST * F, T], [1, F]]),
                               xs[0:ST, bass.ds(g4, T), :]).then_inc(out_done, 16)
                pool.dma_start(bass.AP(tensor=o.tensor, offset=o.offset + T * ST * F, ap=[[F, DUP], [1, F]]),
                               xs[ST:P, bass.ds(g4 + T - 1, 1), :].rearrange("p t f -> p (t f)")
                               ).then_inc(out_done, 16)
            pool.wait_ge(out_done, 16 * 2 * GROUPS)

        @block.tensor
        def _(pe):
            pe.wait_ge(ident_set, 1)
            pe.wait_ge(w_in, 48)
            nc.tensor.transpose(acc[:, 0, 0:F], wraw, ident[:]).then_inc(wT_raw, 1)
            pe.wait_ge(wT_set, 1)
            nc.tensor.matmul(acc[:, 1, 0:2], wT, araw, start=True, stop=True).then_inc(wa_raw, 1)
            pe.wait_ge(y_in, 16 * GROUPS)
            for g in range(GROUPS):
                if g >= 2:
                    pe.wait_ge(yt_set, g - 1)
                for t in range(T):
                    last = nc.tensor.transpose(bT[g % 2][0:C, t * P:(t + 1) * P],
                                               ystage[:, g * T + t, :], ident[:])
                last.then_inc(yt_raw, 1)

            def fill(g, k, lead=False):
                i = k // T
                if k % T == 0:
                    pe.wait_ge(adj_in[i % SLOTS], g * (16 * PIECES // SLOTS) + 16 * (i // SLOTS + 1))
                if not lead:
                    pe.wait_ge(mask_set, g * NT + (k - 1))
                for t in range(T):
                    c = ST * (k % T)
                    last = nc.tensor.transpose(bT[k % 2][:, t * P:(t + 1) * P],
                                               abuf[:, i % SLOTS, t, c:c + P], ident[:])
                last.then_inc(blk_t, 1)

            def labels(g, k):
                nc.tensor.matmul(bY[k % 2][:, :], yt[0:C, k * P:(k + 1) * P], yt[0:C, dsn(g * GW, GW)],
                                 start=True, stop=True).then_inc(blk_y, 1)

            def add(g, k):
                if k == 0:
                    pe.wait_ge(staged_a, g + 1)
                if isinstance(g, int) or k % T == 0:
                    pe.wait_ge(h_set, k // T + 1)
                pe.wait_ge(g_set, g * NT + (k + 1))
                for t in range(T):
                    lhs = gbuf[:, k % 4, t * P:(t + 1) * P]
                    o = t % 2 * (F + 1)
                    nc.tensor.matmul(acc_a[:, t // 2, o:o + F + 1], lhs, hm[:, k, 0, :],
                                     start=(k == 0 and t % 2 == 0), stop=False, skip_group_check=True)
                    last = nc.tensor.matmul(acc_a[:, t // 2, o:o + F], lhs, hm[:, k, 1, 0:F],
                                            start=False, stop=(k == NT - 1), skip_group_check=True)
                last.then_inc(g_used, 1)

            pe.wait_ge(yt_set, GROUPS)
            for k in range(2):
                fill(0, k, True)
                labels(0, k)
            with pe.Fori(0, GROUPS - 1) as g:
                for k in range(NT):
                    ahead = (g if k + 2 < NT else g + 1, (k + 2) % NT)
                    fill(*ahead)
                    add(g, k)
                    labels(*ahead)
            for k in range(NT):
                if k + 2 < NT:
                    fill(GROUPS - 1, k + 2)
                add(GROUPS - 1, k)
                if k + 2 < NT:
                    labels(GROUPS - 1, k + 2)

            pe.wait_ge(staged_a, GROUPS + 1)

            def project(g, v, lead):
                pe.wait_ge(zb_set, g + 1)
                if not lead:
                    pe.wait_ge(ht_set, g - 1)
                for t in range(T):
                    last = nc.tensor.transpose(bT[v][:, t * P:(t + 1) * P], zb[:, v, t, :], ident[:])
                last.then_inc(ht_raw, 1)
                pe.wait_ge(ht_set, g + 1)
                if not lead:
                    pe.wait_ge(wh_out, g - 1)
                for t in range(T):
                    last = nc.tensor.matmul(acc[:, 2 * v + t // 2, t % 2 * (F + 2):(t % 2 + 1) * (F + 2)],
                                            hT[:, v, t * P:(t + 1) * P], wx[:], start=True, stop=True)
                last.then_inc(wh_raw, 1)
                if not lead:
                    pe.wait_ge(f1_out, g - 1)
                nc.tensor.matmul(bY[v][:, :], wa1[:], hT[:, v, :], start=True, stop=True).then_inc(f1_raw, 1)

            project(0, 0, True)
            project(1, 1, True)
            with pe.Fori(1, GROUPS // 2) as u:
                for v in range(2):
                    project(u * 2 + v, v, False)
            pe.wait_ge(hsb_set, 1)
            nc.tensor.matmul(bT[0][:, 0:F], hsb, wx[:, 0:F], start=True, stop=True).then_inc(mean_raw, 1)

            pe.wait_ge(wh_out, GROUPS)
            pe.sem_inc(m_used, 2)
            with pe.Fori(0, GROUPS) as q:
                for k in range(NT):
                    p, j = k // 2, k % 2
                    if k == 0:
                        pe.wait_ge(staged_b, q + 1)
                    if k % T == 0:
                        pe.wait_ge(xm_set, k // T + 1)
                    if j == 0:
                        pe.wait_ge(mp_set, q * PAIRS + (p + 1))
                        pe.wait_ge(mn_set, q * PAIRS + (p + 1))
                    for t in range(T):
                        for m, src in enumerate((mpos, mneg)):
                            lhs = src[:, p % 2, j, t * P:(t + 1) * P]
                            for h in range(2):
                                last = nc.tensor.matmul(
                                    acc_b[:, t, m * (F + 1):(m + 1) * (F + 1)], lhs, xm[:, k, m, h, :],
                                    start=(k == 0 and m == 0 and h == 0), stop=(k == NT - 1 and h == 1),
                                    skip_group_check=True)
                    if j == 1:
                        last.then_inc(m_used, 1)

        @block.scalar
        def _(act):
            act.wait_ge(wT_raw, 1)
            nc.scalar.copy(wT, acc[:, 0, 0:F]).then_inc(wT_set, 1)
            act.wait_ge(wa_raw, 1)
            nc.scalar.copy(wx[:, F:F + 2], acc[:, 1, 0:2]).then_inc(wx_set, 1)
            nc.scalar.copy(wx[:, 0:F], wraw).then_inc(wx_set, 1)
            act.wait_ge(wx_set, 2)
            act.wait_ge(ones_set, 1)
            nc.scalar.activation(wa1[:], ones[:], ACT.Copy, scale=wx[:, F:F + 1]).then_inc(wx_set, 1)
            for g in range(GROUPS):
                act.wait_ge(yt_raw, g + 1)
                nc.scalar.copy(yt[0:C, g * GW:(g + 1) * GW], bT[g % 2][0:C, :]).then_inc(yt_set, 1)
            act.wait_ge(const_set, 2)
            act.wait_ge(var_set, 1)
            nc.scalar.activation(inv[:], mv[:, :, 1], ACT.Sqrt, bias=const[:, 0:1]).then_inc(std_set, 1)
            with act.Fori(0, GROUPS // 2) as u:
                for v in range(2):
                    act.wait_ge(za_set, u * 2 + (v + 1))
                    nc.scalar.activation(hm[:, bass.ds(u * (2 * T) + v * T, T), 0, 0:F], za[:, v],
                                         ACT.Relu, scale=H_SCALE).then_inc(za_split, 1)
                    nc.scalar.activation(za[:, v], za[:, v], ACT.Relu, scale=H_SCALE).then_inc(za_split, 1)

            def byte_mask(g, k):
                if k == 0:
                    act.wait_ge(slot_free, g + 1)
                act.wait_ge(blk_t, g * NT + (k + 1))
                slot = g % HALF
                nc.scalar.activation(mask[:, ds1(slot), k, :].rearrange("p s c -> p (s c)"), bT[k % 2][:, :],
                                     ACT.Copy, scale=2.0).then_inc(mask_set, 1)

            def stage_a(g):
                act.wait_ge(g_used, g * NT + NT)
                act.wait_ge(x1_set, g + 1)
                act.wait_ge(rec_a, g + 1)
                dst = stage[:].rearrange("p t m c -> p (t m c)")[:, 0:T * (F + 1)].rearrange(
                    "p (b c) -> p b c", b=2)
                nc.scalar.copy(dst, acc_a).then_inc(staged_a, 1)

            byte_mask(0, 0)
            byte_mask(0, 1)
            with act.Fori(0, GROUPS - 1) as g:
                for k in range(2, NT):
                    byte_mask(g, k)
                byte_mask(g + 1, 0)
                byte_mask(g + 1, 1)
                stage_a(g)
            for k in range(2, NT):
                byte_mask(GROUPS - 1, k)
            stage_a(GROUPS - 1)

            act.wait_ge(var2_set, 1)
            nc.scalar.activation(inv[:], mv[:, :, 1], ACT.Sqrt, bias=const[:, 0:1]).then_inc(std2_set, 1)

            def evacuate(g, v, lead):
                act.wait_ge(ht_raw, g + 1)
                if not lead:
                    act.wait_ge(f1_raw, g - 1)
                    act.wait_ge(hs_set, g - 1)
                nc.scalar.activation(hT[:, v, :], bT[v][:, :], ACT.Relu).then_inc(ht_set, 1)
                act.wait_ge(f1_raw, g + 1)
                nc.scalar.copy(f1b[:, dsn(g * GW, GW)], bY[v][:, :]).then_inc(f1_out, 1)

            evacuate(0, 0, True)
            evacuate(1, 1, True)
            with act.Fori(1, GROUPS // 2) as u:
                for v in range(2):
                    evacuate(u * 2 + v, v, False)
            act.wait_ge(sm_set, 2)
            nc.scalar.activation(bcol, f2c, ACT.Exp, bias=sm[:, 0:1]).then_inc(bd_set, 1)
            nc.scalar.activation(dcol, f2c, ACT.Exp, bias=sm[:, 1:2], scale=SLOPE).then_inc(bd_set, 1)
            act.wait_ge(row_set, 2)
            nc.scalar.activation(ac, ac, ACT.Exp).then_inc(ac_set, 1)
            nc.scalar.activation(cc, cc, ACT.Exp).then_inc(ac_set, 1)
            with act.Fori(0, GROUPS // 2) as u:
                for v in range(2):
                    act.wait_ge(zx_set, u * 2 + (v + 1))
                    nc.scalar.copy(xm[:, bass.ds(u * (2 * T) + v * T, T), :, 0, :], zx[:, v]).then_inc(zx_hi, 1)

            def positive(q, p):
                act.wait_ge(v_set, q * PAIRS + (p + 1))
                act.wait_ge(m_used, q * PAIRS + (p + 1))
                nc.scalar.activation(mpos[:, p % 2], vbuf[:, p % 2], ACT.Relu, bias=const[:, 1:2]
                                     ).then_inc(mp_set, 1)

            def f1_bank(q):
                act.wait_ge(v_set, q * PAIRS)
                nc.scalar.copy(f1p[:, :], f1b[:, dsn(of_turn(q) * GW, GW)]).then_inc(f1p_set, 1)

            def stage_b(q):
                act.wait_ge(m_used, q * PAIRS + (PAIRS + 2))
                act.wait_ge(stageb_free, q + 1)
                act.wait_ge(rec_b, q + 1)
                nc.scalar.copy(stage[:].rearrange("p t m c -> p t (m c)"), acc_b).then_inc(staged_b, 1)

            f1_bank(0)
            positive(0, 0)
            positive(0, 1)
            with act.Fori(0, GROUPS - 1) as q:
                for p in range(2, PAIRS):
                    positive(q, p)
                f1_bank(q + 1)
                positive(q + 1, 0)
                positive(q + 1, 1)
                stage_b(q)
            for p in range(2, PAIRS):
                positive(GROUPS - 1, p)
            stage_b(GROUPS - 1)

        @block.vector
        def _(dve):
            step = [0]

            def chain(ins):
                step[0] += 1
                ins.then_inc(dve_step, 1)
                dve.wait_ge(dve_step, step[0])

            chain(nc.vector.memset(hm[:, :, 0, F:F + 1], 1.0))
            nc.vector.memset(hm[0:DUP].rearrange("p (g t) h c -> p g t h c", t=T)[:, :, 1:T, 0, F], 0.0)

            def moments(done):
                with dve.Fori(0, GROUPS) as g:
                    for t in range(T):
                        k = g * T + t
                        last = nc.vector.bn_stats(stats[:, bass.ds(k, 1), :].rearrange("p k c -> p (k c)"),
                                                  xs[:, bass.ds(k, 1), :].rearrange("p k c -> p (k c)"))
                    last.then_inc(dve_step, 1)
                step[0] += GROUPS
                dve.wait_ge(dve_step, step[0])
                for k in range(NT):
                    last = nc.vector.bn_aggr(mv[:, k, :], stats[:, k, :])
                chain(last)

            def inverse_std():
                chain(nc.vector.reciprocal(tmp[:], inv[:]))
                chain(nc.vector.scalar_tensor_tensor(tmp[:], mv[:, :, 1], EPS, tmp[:], ALU.add, ALU.mult))
                chain(nc.vector.tensor_tensor(tmp[:], tmp[:], inv[:], ALU.add))
                chain(nc.vector.tensor_scalar(tmp[:], tmp[:], 0.5, None, ALU.mult))
                chain(nc.vector.reciprocal(inv[:], tmp[:]))

            def normalise(dst, g):
                for t in range(T):
                    k = g * T + t
                    last = nc.vector.tensor_scalar(
                        dst[:, t, :], xs[:, ds1(k), :].rearrange("p k c -> p (k c)"),
                        mv[:, ds1(k), 0], inv[:, ds1(k)], ALU.subtract, ALU.mult)
                return last

            dve.wait_ge(x_in, 16 * GROUPS)
            moments(0)
            nc.vector.memset(tmp[:], 0.0).then_inc(var_set, 1)
            dve.wait_ge(std_set, 1)
            inverse_std()
            chain(nc.vector.memset(inv[0:DUP].rearrange("p (g t) -> p g t", t=T)[:, :, 1:T], 0.0))

            def low_a(g, v):
                dve.wait_ge(za_split, g * 2 + 2)
                hg = hm[:, dsn(g * T, T)]
                nc.vector.tensor_tensor(hg[:, :, 1, 0:F], za[:, v], hg[:, :, 0, 0:F], ALU.subtract
                                        ).then_inc(h_set, 1)

            normalise(za[:, 0], 0).then_inc(za_set, 1)
            normalise(za[:, 1], 1).then_inc(za_set, 1)
            with dve.Fori(0, GROUPS // 2 - 1) as u:
                for v in range(2):
                    low_a(u * 2 + v, v)
                    dve.wait_ge(h_set, u * 2 + (v + 1))
                    normalise(za[:, v], u * 2 + (v + 2)).then_inc(za_set, 1)
            low_a(GROUPS - 2, 0)
            low_a(GROUPS - 1, 1)

            stg = stage[:].rearrange("p t m c -> p (t m c)")[:, 0:T * (F + 1)].rearrange(
                "p (t c) -> p t c", t=T)
            REC = step[0]

            def reciprocals_a(g):
                dve.wait_ge(staged_a, g + 1)
                nc.vector.tensor_scalar(rec[:], stg[:, :, F], L1_EPS, H_SCALE / MIX, ALU.max, ALU.mult
                                        ).then_inc(dve_step, 1)
                dve.wait_ge(dve_step, g + (REC + 1))
                nc.vector.reciprocal(rec[:], rec[:]).then_inc(rec_a, 1)

            with dve.Fori(0, GROUPS) as g:
                for k in range(NT):
                    if k == 6:
                        reciprocals_a(g)
                    dve.wait_ge(mask_set, g * NT + (k + 1))
                    dve.wait_ge(blk_y, g * NT + (k + 1))
                    m = mask[:, bass.ds(g % HALF, 1), k, :].rearrange("p s c -> p (s c)")
                    nc.vector.scalar_tensor_tensor(gbuf[:, k % 4, :], m, 0.5, bY[k % 2][:, :],
                                                   ALU.mult, ALU.mult).then_inc(g_set, 1)
            reciprocals_a(GROUPS)
            step[0] += GROUPS + 1

            dve.wait_ge(x1_set, GROUPS + 1)
            moments(1)
            nc.vector.memset(tmp[:], 0.0).then_inc(var2_set, 1)
            dve.wait_ge(std2_set, 1)
            inverse_std()

            def collect(g, v):
                dve.wait_ge(ht_set, g + 1)
                hv = hT[:, v, :].rearrange("p (t c) -> p t c", t=T)
                hs = hsum.rearrange("p (g c) -> p g c", c=2)[:, dsn(g, 1), :].rearrange("p g c -> p (g c)")
                nc.vector.tensor_reduce(hs[:, 0:1], hv[:, :, DUP:P], AX.XY, ALU.add)
                nc.vector.tensor_reduce(hs[:, 1:2], hv[:, 0, 0:DUP], AX.X, ALU.add).then_inc(hs_set, 1)
                dve.wait_ge(wh_raw, g + 1)
                src = acc[:, 2 * v:2 * v + 2, 0:2 * (F + 2)].rearrange("p b (t c) -> p b t c", t=2)
                for b in range(2):
                    k = g * T + 2 * b
                    nc.vector.tensor_copy(wh[:, dsn(k, 2), 0:F], src[:, b, :, 0:F])
                    nc.vector.tensor_copy(f1c[:, dsn(k, 2)], src[:, b, :, F])
                    last = nc.vector.tensor_copy(f2c[:, dsn(k, 2)], src[:, b, :, F + 1])
                last.then_inc(wh_out, 1)

            normalise(zb[:, 0], 0).then_inc(zb_set, 1)
            normalise(zb[:, 1], 1).then_inc(zb_set, 1)
            with dve.Fori(0, GROUPS // 2 - 1) as u:
                for v in range(2):
                    g = u * 2 + v
                    dve.wait_ge(ht_raw, g + 1)
                    normalise(zb[:, v], g + 2).then_inc(zb_set, 1)
                    collect(g, v)
            collect(GROUPS - 2, 0)
            collect(GROUPS - 1, 1)
            dve.wait_ge(wh_out, GROUPS)
            dve.wait_ge(hs_set, GROUPS)
            nc.vector.tensor_reduce(pm[:, 0:1], f2c, AX.X, ALU.max).then_inc(pm_set, 1)
            nc.vector.tensor_reduce(pm[:, 1:2], wh[:, :, 0:F], AX.XY, ALU.max,
                                    apply_absolute_value=True).then_inc(pm_set, 1)
            chain(nc.vector.tensor_reduce(hs1, hsum, AX.X, ALU.add))
            chain(nc.vector.tensor_scalar(hs1, hs1, 1.0 / N, None, ALU.mult))
            dve.wait_ge(ones_set, 1)
            nc.vector.tensor_scalar(hsb, ones[:], hs1, None, ALU.mult).then_inc(hsb_set, 1)
            nc.vector.tensor_scalar(nf2, f2c, -1.0, None, ALU.mult)
            dve.wait_ge(gm_set, 1)
            nc.vector.tensor_scalar(sm[:, 0:1], gm[:, 0:1], -1.0, None, ALU.mult).then_inc(sm_set, 1)
            nc.vector.tensor_scalar(sm[:, 1:2], gm[:, 0:1], -SLOPE, None, ALU.mult).then_inc(sm_set, 1)
            chain(nc.vector.tensor_scalar(sm[:, 2:3], gm[:, 1:2], 1e-30, None, ALU.max))
            chain(nc.vector.reciprocal(sm[:, 3:4], sm[:, 2:3]))
            chain(nc.vector.tensor_scalar(sc, f1c, gm[:, 0:1], None, ALU.add))
            nc.vector.tensor_scalar(ac, sc, 1.0 - SLOPE, 0.0, ALU.mult, ALU.min).then_inc(row_set, 1)
            nc.vector.tensor_scalar(cc, sc, SLOPE - 1.0, 0.0, ALU.mult, ALU.min).then_inc(row_set, 1)
            dve.wait_ge(mean_raw, 1)
            nc.vector.tensor_scalar(mw, bT[0][:, 0:F], sm[:, 3:4], None, ALU.mult).then_inc(mw_set, 1)
            chain(nc.vector.tensor_scalar(wh[:, :, F], f2c, 0.0, sm[:, 2:3], ALU.mult, ALU.add))
            dve.wait_ge(bd_set, 2)
            for colv, scaled in ((bcol, bwc), (dcol, dwc)):
                chain(nc.vector.memset(colv.rearrange("p (g t) -> p g t", t=T)[0:DUP, :, 1:T], 0.0))
                chain(nc.vector.tensor_scalar(scaled, colv, sm[:, 3:4], B_SCALE, ALU.mult, ALU.mult))

            def scale_features(g, v):
                for t in range(T):
                    for m, colv in enumerate((bwc, dwc)):
                        k = g * T + t
                        last = nc.vector.tensor_scalar(
                            zx[:, v, t, m, :], wh[:, ds1(k), :].rearrange("p k c -> p (k c)"),
                            colv[:, ds1(k)], None, ALU.mult)
                last.then_inc(zx_set, 1)

            def low_b(g, v):
                dve.wait_ge(zx_hi, g + 1)
                xg = xm[:, dsn(g * T, T)]
                nc.vector.tensor_tensor(xg[:, :, :, 1, :], zx[:, v], xg[:, :, :, 0, :], ALU.subtract
                                        ).then_inc(xm_set, 1)

            scale_features(0, 0)
            scale_features(1, 1)
            with dve.Fori(0, GROUPS // 2 - 1) as u:
                for v in range(2):
                    low_b(u * 2 + v, v)
                    dve.wait_ge(xm_set, u * 2 + (v + 1))
                    scale_features(u * 2 + (v + 2), v)
            low_b(GROUPS - 2, 0)
            low_b(GROUPS - 1, 1)

            DEN = step[0]
            dve.wait_ge(xm_set, GROUPS)

            def reciprocals_b(q):
                dve.wait_ge(num_b, q + 1)
                d = stage[:, :, 0, F]
                nc.vector.tensor_scalar(den[:, 0, :], d, 0.0, None, ALU.is_equal).then_inc(dve_step, 1)
                dve.wait_ge(dve_step, q * 3 + (DEN + 1))
                nc.vector.tensor_tensor(den[:, 1, :], d, den[:, 0, :], ALU.add).then_inc(dve_step, 1)
                dve.wait_ge(dve_step, q * 3 + (DEN + 2))
                nc.vector.reciprocal(den[:, 1, :], den[:, 1, :]).then_inc(dve_step, 1)
                dve.wait_ge(dve_step, q * 3 + (DEN + 3))
                nc.vector.tensor_scalar(rec[:], den[:, 1, :], sm[:, 2:3], None, ALU.mult).then_inc(rec_b, 1)

            def compare(q, p):
                if p == 0:
                    dve.wait_ge(f1p_set, q + 1)
                for j in range(2):
                    k = 2 * p + j
                    m = mask[:, bass.ds(q % HALF, 1), k, :].rearrange("p s c -> p (s c)")
                    last = nc.vector.scalar_tensor_tensor(vbuf[:, p % 2, j, :], f1p[:, :], nf2[:, k:k + 1], m,
                                                          ALU.is_gt, ALU.add)
                last.then_inc(v_set, 1)

            def negative(q, p):
                dve.wait_ge(v_set, q * PAIRS + (p + 1))
                dve.wait_ge(m_used, q * PAIRS + (p + 1))
                nc.vector.tensor_scalar(mneg[:, p % 2], vbuf[:, p % 2], 2.0, None, ALU.is_equal
                                        ).then_inc(mn_set, 1)

            def turn(q, first=False, back=False):
                for p in range(PAIRS + 1):
                    if p < PAIRS:
                        if p >= 2 or not first:
                            dve.wait_ge(mp_set, q * PAIRS + (p - 1))
                            dve.wait_ge(mn_set, q * PAIRS + (p - 1))
                        if p == 0 and back:
                            dve.wait_ge(reloaded, (q - HALF) * 16 + 16)
                        compare(q, p)
                    if p == 3:
                        reciprocals_b(q)
                    if p > 0:
                        negative(q, p - 1)

            turn(0, first=True)
            with dve.Fori(1, HALF) as q:
                turn(q)
            with dve.Fori(HALF, GROUPS) as q:
                turn(q, back=True)
            reciprocals_b(GROUPS)


_INS = ["x", "adj", "L0_gnn_h0", "L0_gnn_y", "L1_gnn_W", "L1_gnn_a1", "L1_gnn_a2"]


def kernel(**inputs):
    import numpy as _np
    import concourse.bacc as _bacc
    from concourse.bass_utils import run_bass_kernel_spmd as _run

    nc = _bacc.Bacc("TRN2", target_bir_lowering=False, num_devices=1)
    arrays, args = {}, []
    for name in _INS:
        a = _np.ascontiguousarray(inputs[name])
        arrays[f"in_{name}_dram"] = a
        args.append(nc.dram_tensor(f"in_{name}_dram", a.shape, mybir.dt.from_np(a.dtype),
                                   kind="ExternalInput").ap())
    out = nc.dram_tensor("out_0_dram", (N, F), F32, kind="ExternalOutput").ap()
    spill = nc.dram_tensor("mask_spill", (HALF, P, NT * GW), U8, kind="Internal").ap()
    graph_layers(nc, *args, out, spill)
    r = _run(nc, [arrays], core_ids=[0])
    return r.results[0]["out_0_dram"]
```

```python
from contextlib import ExitStack

import concourse.bass as bass
from concourse import mybir

ALU = mybir.AluOpType
ACT = mybir.ActivationFunctionType
F32 = mybir.dt.float32
F16 = mybir.dt.float16
BF16 = mybir.dt.bfloat16
U8 = mybir.dt.uint8
AX = mybir.AxisListType
RMAX = bass.bass_isa.ReduceOp.max

P = 128
N = 5000
F = 128
C = 16
GROUPS = 10
GR = N // GROUPS
T = 4
ST = (GR - P) // (T - 1)
DUP = P - ST
NT = GROUPS * T
GW = T * P
HALF = GROUPS // 2
SLOTS = 5
EPS = 1e-5
L1_EPS = 1e-12
H_SCALE = 1024.0
B_SCALE = 16384.0
SLOPE = 0.2
MIX = 0.9
PAIRS = NT // 2
F1 = F + 1
HT_STEP, WH_STEPS = 23, (25, 27)


def graph_layers(nc, x, adj, h0, y, w, a1, a2, out, spill, f1_dram):
    with ExitStack() as ctx:
        def sb(name, shape, dt=F32):
            return ctx.enter_context(nc.sbuf_tensor(name, shape, dt))

        def sem(name):
            return ctx.enter_context(nc.semaphore(name))

        mask = sb("mask", [P, HALF, NT, GW], U8)
        xs = sb("xs", [P, NT, F])
        stage = sb("stage", [P, T * 2 * F1])
        ident = sb("ident", [P, P])
        identb = sb("identb", [P, P], BF16)
        wx = sb("wx", [P, F + 2])
        mv = sb("mv", [P, NT, 2])
        inv = sb("inv", [P, NT])
        tmp = sb("tmp", [P, NT])
        stats1 = sb("stats1", [P, T, 6])
        mv1 = sb("mv1", [P, T, 2])
        const = sb("const", [P, 8])
        rec = sb("rec", [P, T])
        den = sb("den", [P, 2, T])
        arena = sb("arena", [P, 20880])

        def at(lo, n, dt=F32):
            v = arena[:, lo:lo + n]
            return v if dt == F32 else v.bitcast(dt)

        hm = at(0, 10320, F16).rearrange("p (k c) -> p k c", k=NT)
        wh = at(0, 10320).rearrange("p (k c) -> p k c", k=NT)[:, :, F1:2 * F1]
        xm = at(0, 10320, F16).rearrange("p (k m h c) -> p k m h c", k=NT, m=2, h=2)
        yt = at(10320, 2560, F16)
        abuf = at(12880, 5000, BF16).rearrange("p (s t c) -> p s t c", s=SLOTS, t=T)
        gbuf = at(17880, 1024, F16).rearrange("p (s c) -> p s c", s=4)
        za = at(18904, 1024).rearrange("p (s t c) -> p s t c", s=2, t=T)
        zb = za[:, 0]
        hT = at(19928, 512)
        h0buf = hT.rearrange("p (t c) -> p t c", t=T)
        ystage = at(12880, NT * C).rearrange("p (k c) -> p k c", k=NT)
        wraw = at(13600, F)
        wT = at(13800, F)
        araw = at(14000, 2)
        stats = stage[:, 0:NT * 6].rearrange("p (k c) -> p k c", k=NT)
        f1b = at(10320, 5120)
        vbuf = at(15440, 2048, BF16).rearrange("p (s j c) -> p s j c", s=4, j=2)
        mpos = at(17488, 1024, BF16).rearrange("p (s j c) -> p s j c", s=2, j=2)
        mneg = at(18512, 1024, BF16).rearrange("p (s j c) -> p s j c", s=2, j=2)
        nf2, bcol, dcol, bwc, dwc, sc, ac, cc = (at(19536 + NT * i, NT) for i in range(8))
        mw, hsb, f1t = (at(19860 + P * i, P) for i in range(3))
        pm, gm, sm, hs1 = at(20250, 2), at(20254, 2), at(20258, 8), at(20268, 1)
        f1c, f2c, hsum, top = at(20440, NT), at(20480, NT), at(20520, 2 * GROUPS), at(20540, GROUPS)
        sums_a = stage[:, 0:T * (F + F1)].rearrange("p (t c) -> p t c", t=T)
        sums_b = stage[:, :].rearrange("p (t m c) -> p t m c", t=T, m=2)

        ps = ctx.enter_context(nc.psum_tensor("ps", [P, 8, 512], F32))
        bT = [ps[:, b, :].bitcast(BF16)[:, 0:GW] for b in (0, 1)]
        bP = ps[:, 1, :]
        bY = [ps[:, b, :] for b in (2, 3)]
        acc_a = ps[:, 4:8, 0:F + F1]
        acc_b = ps[:, :, 0:2 * F1].rearrange("p (t m) c -> p t m c", m=2)

        x_in = [sem(f"x_in{g}") for g in range(GROUPS)]
        y_in, w_in = sem("y_in"), sem("w_in")
        const_set, ident_set, identb_set = sem("const_set"), sem("ident_set"), sem("identb_set")
        dve_step, pool_step = sem("dve_step"), sem("pool_step")
        yt_raw, yt_set = sem("yt_raw"), sem("yt_set")
        wT_raw, wT_set, wa_raw, wx_set = sem("wT_raw"), sem("wT_set"), sem("wa_raw"), sem("wx_set")
        var_set, std_set = sem("var_set"), sem("std_set")
        za_set, za_split, h_set = sem("za_set"), sem("za_split"), sem("h_set")
        h0_in, h0_added = sem("h0_in"), sem("h0_added")
        adj_in = [sem(f"adj_in{i}") for i in range(SLOTS)]
        blk_t, blk_y = sem("blk_t"), sem("blk_y")
        mask_set, g_set, g_used = sem("mask_set"), sem("g_set"), sem("g_used")
        staged_a, x1_set, spilled = sem("staged_a"), sem("x1_set"), sem("spilled")
        var1_set, std1_set, zb_set = sem("var1_set"), sem("std1_set"), sem("zb_set")
        ht_raw, ht_set, wh_raw, wh_out = sem("ht_raw"), sem("ht_set"), sem("wh_raw"), sem("wh_out")
        hs_set, f1t_raw, f1t_set, f1_out, f1_in = (
            sem("hs_set"), sem("f1t_raw"), sem("f1t_set"), sem("f1_out"), sem("f1_in"))
        hsb_set, mean_raw, mw_set = sem("hsb_set"), sem("mean_raw"), sem("mw_set")
        pm_set, gm_set, sm_set, bd_set = sem("pm_set"), sem("gm_set"), sem("sm_set"), sem("bd_set")
        row_set, ac_set, bw_set = sem("row_set"), sem("ac_set"), sem("bw_set")
        zx_set, zx_hi, xm_set = sem("zx_set"), sem("zx_hi"), sem("xm_set")
        reloaded, v_set = sem("reloaded"), sem("v_set")
        mp_set, mn_set, m_used = sem("mp_set"), sem("mn_set"), sem("m_used")
        lo_set, staged_b, num_b, rec_b, stage_free = (
            sem("lo_set"), sem("staged_b"), sem("num_b"), sem("rec_b"), sem("stage_free"))
        prep, top_set = sem("prep"), sem("top_set")
        out_ready, out_done, relu_turn = sem("out_ready"), sem("out_done"), sem("relu_turn")
        dve_turn = sem("dve_turn")

        def rows(src, row0, width, col0=0, ncols=None):
            v = src[bass.ds(row0, GR), :] if not isinstance(row0, int) else src[row0:row0 + GR, :]
            return bass.AP(tensor=v.tensor, offset=v.offset + col0,
                           ap=[[width, P], [ST * width, T], [1, ncols or width]])

        def of_turn(q):
            return (q + HALF) % GROUPS

        def dsn(i, n):
            return slice(i, i + n) if isinstance(i, int) else bass.ds(i, n)

        def one(v, i):
            return v[:, dsn(i, 1)].rearrange("p k c -> p (k c)")

        block = ctx.enter_context(nc.Block())

        @block.sync
        def _(sp):
            for g in range(GROUPS):
                sp.dma_start(xs[:, g * T:(g + 1) * T, :], rows(x, g * GR, F)).then_inc(x_in[g], 16)
            for g in range(GROUPS):
                if g:
                    sp.wait_ge(h0_added, g)
                sp.dma_start(h0buf, rows(h0, g * GR, F)).then_inc(h0_in, 16)
            for s in range(HALF):
                sp.wait_ge(mask_set, (s + 1) * NT)
                sp.dma_start(spill[s], mask[:, s].rearrange("p k c -> p (k c)")).then_inc(spilled, 16)
                sp.wait_ge(spilled, (s + 1) * 16)
            sp.wait_ge(f1t_set, 1)
            sp.dma_start(f1_dram, f1t[0:NT, :]).then_inc(f1_out, 16)
            sp.wait_ge(f1_out, 16)
            for g in (HALF, 0):
                flat = f1_dram[g * T:(g + HALF) * T, :]
                sp.dma_start(f1b[:, g * GW:(g + HALF) * GW],
                             bass.AP(tensor=flat.tensor, offset=flat.offset, ap=[[0, P], [1, HALF * GW]])
                             ).then_inc(f1_in, 16)
                sp.wait_ge(f1_in, 16 if g else 32)
            for q in range(GROUPS):
                if q < HALF:
                    sp.wait_ge(v_set, (q + 1) * PAIRS)
                    sp.dma_start(mask[:, q].rearrange("p k c -> p (k c)"), spill[q]).then_inc(reloaded, 16)
                    sp.wait_ge(reloaded, (q + 1) * 16)
                if q == HALF - 1:
                    done = range(HALF)
                elif q >= HALF:
                    done = (q,)
                else:
                    done = ()
                for d in done:
                    sp.wait_ge(out_ready, d + 1)
                    g = (d + HALF) % GROUPS
                    o = out[g * GR:(g + 1) * GR, :]
                    sp.dma_start(bass.AP(tensor=o.tensor, offset=o.offset,
                                         ap=[[F, ST], [ST * F, T], [1, F]]),
                                 xs[0:ST, g * T:(g + 1) * T, :]).then_inc(out_done, 16)
                    sp.dma_start(out[g * GR + T * ST:(g + 1) * GR, :], xs[ST:P, g * T + T - 1, :]
                                 ).then_inc(out_done, 16)
            sp.wait_ge(out_done, 16 * 2 * GROUPS)

        @block.gpsimd
        def _(pool):
            nc.gpsimd.memset(ident[:], 0.0).then_inc(pool_step, 1)
            nc.gpsimd.memset(identb[:], 0.0).then_inc(pool_step, 1)
            nc.gpsimd.memset(const[:, 0:1], EPS).then_inc(const_set, 1)
            nc.gpsimd.memset(const[:, 1:2], -2.0).then_inc(const_set, 1)
            pool.wait_ge(pool_step, 2)
            for i, done in ((ident, ident_set), (identb, identb_set)):
                nc.gpsimd.affine_select(out=i[:], in_=i[:], compare_op=ALU.not_equal, fill=1.0,
                                        base=0, pattern=[[-1, P]], channel_multiplier=1).then_inc(done, 1)
            pool.wait_ge(yt_raw, GROUPS)
            pool.wait_ge(wx_set, 2)

            def load(g, i):
                pool.dma_start(abuf[:, i % SLOTS], rows(adj, g * GR, N, i * GR, GR)
                               ).then_inc(adj_in[i % SLOTS], 16)

            for i in range(SLOTS):
                load(0, i)
            with pool.Fori(0, GROUPS - 1) as g:
                for i in range(GROUPS):
                    pool.wait_ge(blk_t, g * NT + (i + 1) * T)
                    load(g if i + SLOTS < GROUPS else g + 1, (i + SLOTS) % GROUPS)
            for i in range(SLOTS):
                pool.wait_ge(blk_t, (GROUPS - 1) * NT + (i + 1) * T)
                load(GROUPS - 1, i + SLOTS)

            pool.wait_ge(pm_set, 2)
            nc.gpsimd.partition_all_reduce(gm, pm, P, RMAX).then_inc(gm_set, 1)
            pool.wait_ge(bw_set, 1)
            for c in range(GROUPS):
                if c:
                    pool.wait_ge(xm_set, c)
                for m, colv in enumerate((bwc, dwc)):
                    nc.gpsimd.tensor_tensor(
                        sums_b[:, :, m, :], wh[:, c * T:(c + 1) * T, :],
                        colv[:, c * T:(c + 1) * T].unsqueeze(2).to_broadcast([P, T, F1]),
                        ALU.mult).then_inc(zx_set, 1)
            pool.wait_ge(xm_set, GROUPS)
            pool.sem_inc(stage_free, 1)
            pool.wait_ge(ac_set, 2)
            pool.wait_ge(mw_set, 1)
            with pool.Fori(0, GROUPS) as q:
                pool.wait_ge(staged_b, q * T + T)
                g4 = of_turn(q) * T
                for m, colv in enumerate((ac, cc)):
                    nc.gpsimd.tensor_tensor(
                        sums_b[:, :, m, :], sums_b[:, :, m, :],
                        colv[:, bass.ds(g4, T)].unsqueeze(2).to_broadcast([P, T, F1]),
                        ALU.mult).then_inc(pool_step, 1)
                pool.wait_ge(pool_step, q * 6 + 4)
                nc.gpsimd.tensor_tensor(sums_b[:, :, 0, :], sums_b[:, :, 0, :], sums_b[:, :, 1, :],
                                        ALU.add).then_inc(num_b, 1)
                pool.wait_ge(rec_b, q + 1)
                nc.gpsimd.tensor_tensor(sums_b[:, :, 1, 0:F], mw.unsqueeze(1).to_broadcast([P, T, F]),
                                        den[:, 0, :].unsqueeze(2).to_broadcast([P, T, F]), ALU.mult
                                        ).then_inc(pool_step, 1)
                pool.wait_ge(pool_step, q * 6 + 5)
                nc.gpsimd.tensor_tensor(sums_b[:, :, 0, 0:F], sums_b[:, :, 0, 0:F],
                                        sums_b[:, :, 1, 0:F], ALU.add).then_inc(pool_step, 1)
                pool.wait_ge(pool_step, q * 6 + 6)
                nc.gpsimd.tensor_tensor(sums_b[:, :, 0, 0:F], sums_b[:, :, 0, 0:F],
                                        rec[:].unsqueeze(2).to_broadcast([P, T, F]), ALU.mult
                                        ).then_inc(pool_step, 1)
                pool.wait_ge(pool_step, q * 6 + 7)
                pool.sem_inc(relu_turn, 1)
                nc.gpsimd.tensor_scalar(sums_b[:, :, 0, 0:F], sums_b[:, :, 0, 0:F], 0.0, None, ALU.max
                                        ).then_inc(pool_step, 1)
                pool.wait_ge(pool_step, q * 6 + 8)
                xg = xs[:, bass.ds(g4, T), :]
                nc.gpsimd.tensor_tensor(xg, xg, sums_b[:, :, 0, 0:F], ALU.add).then_inc(out_ready, 1)
                pool.wait_ge(out_ready, q + 1)
                pool.sem_inc(stage_free, 1)

        @block.tensor
        def _(pe):
            pe.wait_ge(ident_set, 1)
            pe.wait_ge(y_in, 16 * GROUPS)
            for g in range(GROUPS):
                if g >= 2:
                    pe.wait_ge(yt_set, g - 1)
                for t in range(T):
                    last = nc.tensor.transpose(ps[0:C, g % 2, t * P:(t + 1) * P],
                                               ystage[:, g * T + t, :], ident[:])
                last.then_inc(yt_raw, 1)
            pe.wait_ge(w_in, 48)
            nc.tensor.transpose(ps[:, 4, 0:F], wraw, ident[:]).then_inc(wT_raw, 1)
            pe.wait_ge(wT_set, 1)
            nc.tensor.matmul(ps[:, 5, 0:2], wT, araw, start=True, stop=True).then_inc(wa_raw, 1)

            def fill(g, k, lead=False):
                i = k // T
                if k % T == 0:
                    pe.wait_ge(adj_in[i % SLOTS], g * (16 * GROUPS // SLOTS) + 16 * (i // SLOTS + 1))
                if not lead:
                    pe.wait_ge(mask_set, g * NT + (k - 1))
                for t in range(T):
                    c = ST * (k % T)
                    last = nc.tensor.transpose(bT[k % 2][:, t * P:(t + 1) * P],
                                               abuf[:, i % SLOTS, t, c:c + P], identb[:])
                last.then_inc(blk_t, 1)

            def labels(g, k):
                nc.tensor.matmul(bY[k % 2], yt[0:C, k * P:(k + 1) * P], yt[0:C, dsn(g * GW, GW)],
                                 start=True, stop=True).then_inc(blk_y, 1)

            def add(g, k, first):
                if first and k % T == 0:
                    pe.wait_ge(h_set, k // T + 1)
                pe.wait_ge(g_set, g * NT + (k + 1))
                for t in range(T):
                    if k == 0 and not first and t % 2 == 0:
                        pe.wait_ge(staged_a, g * 2 + (t // 2 - 1))
                    last = nc.tensor.matmul(acc_a[:, t, :], gbuf[:, k % 4, t * P:(t + 1) * P],
                                            hm[:, k, 0:F + F1], start=(k == 0), stop=(k == NT - 1))
                last.then_inc(g_used, 1)

            def transpose_h(p):
                pe.wait_ge(zb_set, p + 1)
                for t in range(T):
                    last = nc.tensor.transpose(bP[:, t * P:(t + 1) * P], zb[:, t, :], ident[:])
                last.then_inc(ht_raw, 1)

            def project(p, part):
                for i in range(2):
                    t = 2 * part + i
                    last = nc.tensor.matmul(bP[:, i * (F + 2):(i + 1) * (F + 2)], hT[:, t * P:(t + 1) * P],
                                            wx[:], start=True, stop=True)
                last.then_inc(wh_raw, 1)

            def group_a(g, first=False, final=False):
                for k in range(NT):
                    special = not first and k in (HT_STEP, *WH_STEPS)
                    if special:
                        pe.wait_ge(mask_set, g * NT + (k + 1))
                        if k == HT_STEP:
                            transpose_h(g - 1)
                        else:
                            project(g - 1, WH_STEPS.index(k))
                        add(g, k, first)
                        if k == HT_STEP:
                            pe.wait_ge(ht_set, g)
                        else:
                            pe.wait_ge(wh_out, g * 2 + (WH_STEPS.index(k) - 1))
                    ahead = (g if k + 2 < NT else g + 1, (k + 2) % NT)
                    going = not (final and k + 2 >= NT)
                    if going:
                        fill(*ahead)
                    if not special:
                        add(g, k, first)
                    if going:
                        labels(*ahead)

            pe.wait_ge(identb_set, 1)
            pe.wait_ge(yt_set, GROUPS)
            for k in range(2):
                fill(0, k, True)
                labels(0, k)
            group_a(0, first=True)
            with pe.Fori(1, GROUPS - 1) as g:
                group_a(g)
            group_a(GROUPS - 1, final=True)

            pe.wait_ge(mask_set, GROUPS * NT)
            transpose_h(GROUPS - 1)
            pe.wait_ge(ht_set, GROUPS)
            for part in range(2):
                project(GROUPS - 1, part)
                pe.wait_ge(wh_out, GROUPS * 2 + part - 1)
            nc.tensor.transpose(ps[0:NT, 0, 0:P], f1c, ident[:]).then_inc(f1t_raw, 1)
            pe.wait_ge(hsb_set, 1)
            nc.tensor.matmul(ps[:, 2, 0:F], hsb, wx[:, 0:F], start=True, stop=True).then_inc(mean_raw, 1)
            pe.wait_ge(f1t_set, 1)
            pe.wait_ge(mw_set, 1)
            pe.wait_ge(staged_a, GROUPS * 2)

            def turn(q, first=False):
                for k in range(NT):
                    p, j = k // 2, k % 2
                    if first and k % T == 0:
                        pe.wait_ge(xm_set, k // T + 1)
                    if j == 0:
                        pe.wait_ge(mp_set, q * PAIRS + (p + 1))
                        pe.wait_ge(mn_set, q * PAIRS + (p + 1))
                    for t in range(T):
                        if k == 0 and not first:
                            pe.wait_ge(staged_b, q * T + (t - T + 1))
                        for m, src in enumerate((mpos, mneg)):
                            last = nc.tensor.matmul(acc_b[:, t, m, :], src[:, p % 2, j, t * P:(t + 1) * P],
                                                    xm[:, k, m].rearrange("p h c -> p (h c)"),
                                                    start=(k == 0), stop=(k == NT - 1))
                    if j == 1:
                        last.then_inc(m_used, 1)

            turn(0, first=True)
            with pe.Fori(1, GROUPS) as q:
                turn(q)

        @block.scalar
        def _(act):
            act.dma_start(wraw, w).then_inc(w_in, 16)
            act.dma_start(araw[:, 0:1], a1).then_inc(w_in, 16)
            act.dma_start(araw[:, 1:2], a2).then_inc(w_in, 16)
            for g in range(GROUPS):
                act.dma_start(ystage[:, g * T:(g + 1) * T, :], rows(y, g * GR, C)).then_inc(y_in, 16)
            for g in range(GROUPS):
                act.wait_ge(yt_raw, g + 1)
                nc.scalar.copy(yt[0:C, g * GW:(g + 1) * GW], ps[0:C, g % 2, :]).then_inc(yt_set, 1)
            act.wait_ge(wT_raw, 1)
            nc.scalar.copy(wT, ps[:, 4, 0:F]).then_inc(wT_set, 1)
            act.wait_ge(wa_raw, 1)
            nc.scalar.copy(wx[:, F:F + 2], ps[:, 5, 0:2]).then_inc(wx_set, 1)
            nc.scalar.copy(wx[:, 0:F], wraw).then_inc(wx_set, 1)
            act.wait_ge(const_set, 2)
            act.wait_ge(var_set, 1)
            nc.scalar.activation(inv[:], mv[:, :, 1], ACT.Sqrt, bias=const[:, 0:1]).then_inc(std_set, 1)

            def split_h(c):
                act.wait_ge(za_set, c + 1)
                nc.scalar.activation(hm[:, c * T:(c + 1) * T, 0:F], za[:, c % 2], ACT.Relu, scale=H_SCALE
                                     ).then_inc(za_split, 1)
                nc.scalar.activation(za[:, c % 2], za[:, c % 2], ACT.Relu, scale=H_SCALE
                                     ).then_inc(za_split, 1)

            def stage_a(p):
                act.wait_ge(g_used, p * NT + NT)
                for b in range(2):
                    nc.scalar.copy(sums_a[:, 2 * b:2 * b + 2, :], acc_a[:, 2 * b:2 * b + 2, :]
                                   ).then_inc(staged_a, 1)

            def deviation(p):
                act.wait_ge(var1_set, p + 1)
                nc.scalar.activation(inv[:, dsn(p * T, T)], mv[:, dsn(p * T, T), 1], ACT.Sqrt,
                                     bias=const[:, 0:1]).then_inc(std1_set, 1)

            def relu_h(p):
                act.wait_ge(ht_raw, p + 1)
                nc.scalar.activation(hT, bP, ACT.Relu).then_inc(ht_set, 1)

            def group_a(g, first=False, over=False):
                for k in range(NT):
                    if k == 0 and over:
                        act.wait_ge(spilled, g * 16 - 16 * (HALF - 1))
                    act.wait_ge(blk_t, g * NT + (k + 1))
                    nc.scalar.activation(mask[:, dsn(g % HALF, 1), k, :].rearrange("p s c -> p (s c)"),
                                         bT[k % 2], ACT.Copy, scale=2.0).then_inc(mask_set, 1)
                    if first and k % T == 1 and k // T + 1 < GROUPS:
                        split_h(k // T + 1)
                    if not first:
                        if k == 1:
                            stage_a(g - 1)
                        if k == 13:
                            deviation(g - 1)
                        if k == HT_STEP + 1:
                            relu_h(g - 1)

            split_h(0)
            group_a(0, first=True)
            with act.Fori(1, HALF) as g:
                group_a(g)
            with act.Fori(HALF, GROUPS) as g:
                group_a(g, over=True)
            stage_a(GROUPS - 1)
            deviation(GROUPS - 1)
            relu_h(GROUPS - 1)

            act.wait_ge(f1t_raw, 1)
            nc.scalar.copy(f1t[0:NT, :], ps[0:NT, 0, 0:P]).then_inc(f1t_set, 1)
            act.wait_ge(sm_set, 2)
            nc.scalar.activation(bcol, f2c, ACT.Exp, bias=sm[:, 0:1]).then_inc(bd_set, 1)
            nc.scalar.activation(dcol, f2c, ACT.Exp, bias=sm[:, 1:2], scale=SLOPE).then_inc(bd_set, 1)

            def hi_features(c):
                act.wait_ge(zx_set, 2 * c + 2)
                nc.scalar.copy(xm[:, c * T:(c + 1) * T, :, 0, :], sums_b).then_inc(zx_hi, 1)

            def positive(q, p, first):
                act.wait_ge(v_set, q * PAIRS + (p + 1))
                if p >= 2 or not first:
                    act.wait_ge(m_used, q * PAIRS + (p - 1))
                nc.scalar.activation(mpos[:, p % 2], vbuf[:, p % 4], ACT.Relu, bias=const[:, 1:2]
                                     ).then_inc(mp_set, 1)

            def low_sums(q):
                act.wait_ge(m_used, q * PAIRS + PAIRS)
                act.wait_ge(stage_free, q + 1)
                for t in range(T):
                    nc.scalar.copy(sums_b[:, t], acc_b[:, t, :, F1:2 * F1]).then_inc(lo_set, 1)

            def turn(q, first=False):
                for p in range(PAIRS):
                    positive(q, p, first)
                    if p == 0 and not first:
                        low_sums(q - 1)
                    if first and p % 2 == 0 and p // 2 + 1 < GROUPS:
                        hi_features(p // 2 + 1)
                    if first and p == 1:
                        act.wait_ge(row_set, 2)
                        nc.scalar.activation(ac, ac, ACT.Exp).then_inc(ac_set, 1)
                        nc.scalar.activation(cc, cc, ACT.Exp).then_inc(ac_set, 1)

            hi_features(0)
            turn(0, first=True)
            with act.Fori(1, GROUPS) as q:
                turn(q)
            low_sums(GROUPS - 1)

        @block.vector
        def _(dve):
            step = [0]

            def chain(ins):
                step[0] += 1
                ins.then_inc(dve_step, 1)
                dve.wait_ge(dve_step, step[0])

            chain(nc.vector.memset(hm[:, :, F:F1], 1.0))
            nc.vector.memset(hm[0:DUP].rearrange("p (g t) c -> p g t c", t=T)[:, :, 1:T, F], 0.0)

            for g in range(GROUPS):
                dve.wait_ge(x_in[g], 16)
                for k in range(g * T, g * T + T):
                    last = nc.vector.bn_stats(stats[:, k, :], xs[:, k, :])
            chain(last)
            for k in range(NT):
                last = nc.vector.bn_aggr(mv[:, k, :], stats[:, k, :])
            last.then_inc(var_set, 1)
            dve.wait_ge(std_set, 1)

            def newton(lo, n):
                i, t, v = inv[:, dsn(lo, n)], tmp[:, 0:n], mv[:, dsn(lo, n), 1]
                yield nc.vector.reciprocal(t, i)
                yield nc.vector.scalar_tensor_tensor(t, v, EPS, t, ALU.add, ALU.mult)
                yield nc.vector.tensor_tensor(t, t, i, ALU.add)
                yield nc.vector.tensor_scalar(t, t, 0.5, None, ALU.mult)
                yield nc.vector.reciprocal(i, t)

            for ins in newton(0, NT):
                chain(ins)
            chain(nc.vector.memset(inv[0:DUP].rearrange("p (g t) -> p g t", t=T)[:, :, 1:T], 0.0))

            def normalise(dst, g):
                for t in range(T):
                    k = g * T + t
                    last = nc.vector.tensor_scalar(dst[:, t, :], one(xs, k), mv[:, dsn(k, 1), 0],
                                                   inv[:, dsn(k, 1)], ALU.subtract, ALU.mult)
                return last

            def low_h(c):
                dve.wait_ge(za_split, 2 * c + 2)
                hg = hm[:, c * T:(c + 1) * T]
                nc.vector.tensor_tensor(hg[:, :, F1:F + F1], za[:, c % 2], hg[:, :, 0:F], ALU.subtract
                                        ).then_inc(h_set, 1)
                if c + 1 < GROUPS:
                    if c:
                        dve.wait_ge(h_set, c)
                    normalise(za[:, (c + 1) % 2], c + 1).then_inc(za_set, 1)

            def add_h0(c):
                dve.wait_ge(h0_in, 16 * (c + 1))
                dve.wait_ge(za_set, c + 1)
                xg = xs[:, c * T:(c + 1) * T, :]
                nc.vector.scalar_tensor_tensor(
                    xg.rearrange("p t c -> p (t c)"), hT, 1.0 - MIX, xg.rearrange("p t c -> p (t c)"),
                    ALU.mult, ALU.add).then_inc(h0_added, 1)

            def recip(p):
                dve.wait_ge(staged_a, p * 2 + 2)
                nc.vector.tensor_scalar(rec[:], sums_a[:, :, F], L1_EPS, H_SCALE / MIX, ALU.max, ALU.mult
                                        ).then_inc(prep, 1)
                nc.vector.tensor_tensor(sums_a[:, :, 0:F], sums_a[:, :, 0:F], sums_a[:, :, F1:F + F1],
                                        ALU.add).then_inc(prep, 1)

            def recip2(p):
                dve.wait_ge(prep, p * PREP + 1)
                nc.vector.reciprocal(rec[:], rec[:]).then_inc(prep, 1)

            def update(p, lo):
                dve.wait_ge(prep, p * PREP + 3)
                for t in (lo, lo + 1):
                    xk = one(xs, p * T + t)
                    last = nc.vector.scalar_tensor_tensor(xk, sums_a[:, t, 0:F], rec[:, t:t + 1], xk,
                                                          ALU.mult, ALU.add)
                last.then_inc(x1_set, 1)

            def moments(p, lo):
                dve.wait_ge(x1_set, p * 2 + 1 + lo // 2)
                dve.sem_inc(dve_turn, 1)
                for t in (lo, lo + 1):
                    last = nc.vector.bn_stats(stats1[:, t, :], one(xs, p * T + t))
                last.then_inc(prep, 1)

            def gather(p):
                dve.wait_ge(prep, p * PREP + 5)
                dve.sem_inc(dve_turn, 1)
                for t in range(T):
                    last = nc.vector.bn_aggr(mv1[:, t, :], stats1[:, t, :])
                last.then_inc(prep, 1)

            def keep(p):
                dve.wait_ge(prep, p * PREP + 6)
                nc.vector.tensor_copy(mv[:, dsn(p * T, T), :], mv1[:, :, :]).then_inc(var1_set, 1)

            def newton_step(p, i):
                if i == 0:
                    dve.wait_ge(std1_set, p + 1)
                else:
                    dve.wait_ge(prep, p * PREP + (6 + i))
                dve.sem_inc(dve_turn, 1)
                for n, make in enumerate(NEWTON):
                    if n == i:
                        make(inv[:, dsn(p * T, T)], tmp[:, 0:T], mv[:, dsn(p * T, T), 1]).then_inc(prep, 1)

            NEWTON = (
                lambda i, t, v: nc.vector.reciprocal(t, i),
                lambda i, t, v: nc.vector.scalar_tensor_tensor(t, v, EPS, t, ALU.add, ALU.mult),
                lambda i, t, v: nc.vector.tensor_tensor(t, t, i, ALU.add),
                lambda i, t, v: nc.vector.tensor_scalar(t, t, 0.5, None, ALU.mult),
                lambda i, t, v: nc.vector.reciprocal(i, t),
            )
            PREP = 11

            def rows_h(p):
                dve.wait_ge(prep, p * PREP + PREP)
                normalise(zb, p).then_inc(zb_set, 1)

            def sum_h(p):
                dve.wait_ge(ht_set, p + 1)
                hv = hT.rearrange("p (t c) -> p t c", t=T)
                nc.vector.tensor_reduce(hsum[:, dsn(p * 2, 1)], hv[:, :, DUP:P], AX.XY, ALU.add)
                nc.vector.tensor_reduce(hsum[:, dsn(p * 2 + 1, 1)], hv[:, 0, 0:DUP], AX.X, ALU.add
                                        ).then_inc(hs_set, 1)

            def collect(p, part):
                dve.wait_ge(wh_raw, p * 2 + (part + 1))
                v = bP[:, 0:2 * (F + 2)].rearrange("p (t c) -> p t c", t=2)
                k = p * T + 2 * part
                nc.vector.tensor_copy(wh[:, dsn(k, 2), 0:F], v[:, :, 0:F])
                nc.vector.tensor_copy(f1c[:, dsn(k, 2)], v[:, :, F])
                nc.vector.tensor_copy(f2c[:, dsn(k, 2)], v[:, :, F + 1]).then_inc(wh_out, 1)

            def largest(p):
                dve.wait_ge(wh_out, p * 2 + 2)
                nc.vector.tensor_reduce(top[:, dsn(p, 1)], wh[:, dsn(p * T, T), 0:F], AX.XY, ALU.max,
                                        apply_absolute_value=True).then_inc(top_set, 1)

            PARTS = {
                4: lambda p: recip(p), 5: lambda p: recip2(p), 6: lambda p: update(p, 0),
                7: lambda p: update(p, 2), 8: lambda p: moments(p, 0), 9: lambda p: moments(p, 2),
                10: lambda p: gather(p), 11: lambda p: keep(p),
                15: lambda p: newton_step(p, 0), 16: lambda p: newton_step(p, 1),
                17: lambda p: newton_step(p, 2), 18: lambda p: newton_step(p, 3),
                19: lambda p: newton_step(p, 4), 20: lambda p: rows_h(p),
                HT_STEP + 2: lambda p: sum_h(p), WH_STEPS[0] + 1: lambda p: collect(p, 0),
                WH_STEPS[1] + 1: lambda p: collect(p, 1), WH_STEPS[1] + 3: lambda p: largest(p),
            }

            def group_a(g, first=False):
                for k in range(NT):
                    if first and k % T == 0 and k:
                        low_h(k // T)
                    dve.wait_ge(mask_set, g * NT + (k + 1))
                    dve.wait_ge(blk_y, g * NT + (k + 1))
                    m = mask[:, dsn(g % HALF, 1), k, :].rearrange("p s c -> p (s c)")
                    nc.vector.scalar_tensor_tensor(gbuf[:, k % 4, :], m, 0.5, bY[k % 2],
                                                   ALU.mult, ALU.mult).then_inc(g_set, 1)
                    if first and k % T == 2:
                        add_h0(k // T)
                    if not first and k in PARTS:
                        PARTS[k](g - 1)

            normalise(za[:, 0], 0).then_inc(za_set, 1)
            low_h(0)
            group_a(0, first=True)
            with dve.Fori(1, GROUPS) as g:
                group_a(g)
            for k in sorted(PARTS):
                PARTS[k](GROUPS - 1)

            dve.wait_ge(wh_out, 2 * GROUPS)
            dve.wait_ge(hs_set, GROUPS)
            dve.wait_ge(top_set, GROUPS)
            nc.vector.tensor_reduce(pm[:, 0:1], f2c, AX.X, ALU.max).then_inc(pm_set, 1)
            nc.vector.tensor_reduce(pm[:, 1:2], top, AX.X, ALU.max).then_inc(pm_set, 1)
            chain(nc.vector.tensor_reduce(hs1, hsum, AX.X, ALU.add))
            chain(nc.vector.tensor_scalar(hs1, hs1, 1.0 / N, None, ALU.mult))
            nc.vector.tensor_scalar(hsb, ident[:], 0.0, hs1, ALU.mult, ALU.add).then_inc(hsb_set, 1)
            nc.vector.tensor_scalar(nf2, f2c, -1.0, None, ALU.mult)
            dve.wait_ge(gm_set, 1)
            nc.vector.tensor_scalar(sm[:, 0:1], gm[:, 0:1], -1.0, None, ALU.mult).then_inc(sm_set, 1)
            nc.vector.tensor_scalar(sm[:, 1:2], gm[:, 0:1], -SLOPE, None, ALU.mult).then_inc(sm_set, 1)
            chain(nc.vector.tensor_scalar(sm[:, 2:3], gm[:, 1:2], 1e-30, None, ALU.max))
            chain(nc.vector.reciprocal(sm[:, 3:4], sm[:, 2:3]))
            nc.vector.tensor_scalar(wh[:, :, F], f2c, 0.0, sm[:, 2:3], ALU.mult, ALU.add)
            chain(nc.vector.tensor_scalar(sc, f1c, gm[:, 0:1], None, ALU.add))
            nc.vector.tensor_scalar(ac, sc, 1.0 - SLOPE, 0.0, ALU.mult, ALU.min).then_inc(row_set, 1)
            nc.vector.tensor_scalar(cc, sc, SLOPE - 1.0, 0.0, ALU.mult, ALU.min).then_inc(row_set, 1)
            dve.wait_ge(bd_set, 2)
            for colv in (bcol, dcol):
                chain(nc.vector.memset(colv.rearrange("p (g t) -> p g t", t=T)[0:DUP, :, 1:T], 0.0))
            nc.vector.tensor_scalar(bwc, bcol, sm[:, 3:4], B_SCALE, ALU.mult, ALU.mult)
            nc.vector.tensor_scalar(dwc, dcol, sm[:, 3:4], B_SCALE, ALU.mult, ALU.mult).then_inc(bw_set, 1)
            dve.wait_ge(mean_raw, 1)
            nc.vector.tensor_scalar(mw, ps[:, 2, 0:F], sm[:, 3:4], None, ALU.mult).then_inc(mw_set, 1)

            def low_features(c):
                dve.wait_ge(zx_hi, c + 1)
                xg = xm[:, c * T:(c + 1) * T]
                nc.vector.tensor_tensor(xg[:, :, :, 1, :], sums_b, xg[:, :, :, 0, :], ALU.subtract
                                        ).then_inc(xm_set, 1)

            DEN = step[0]

            def reciprocals_b(q):
                dve.wait_ge(num_b, q + 1)
                d = sums_b[:, :, 0, F]
                nc.vector.tensor_scalar(den[:, 0, :], d, 0.0, None, ALU.is_equal).then_inc(dve_step, 1)
                dve.wait_ge(dve_step, q * 3 + (DEN + 1))
                nc.vector.tensor_tensor(den[:, 1, :], d, den[:, 0, :], ALU.add).then_inc(dve_step, 1)
                dve.wait_ge(dve_step, q * 3 + (DEN + 2))
                nc.vector.reciprocal(den[:, 1, :], den[:, 1, :]).then_inc(dve_step, 1)
                dve.wait_ge(dve_step, q * 3 + (DEN + 3))
                nc.vector.tensor_scalar(rec[:], den[:, 1, :], sm[:, 2:3], None, ALU.mult).then_inc(rec_b, 1)

            def full_sums(q):
                for t in range(T):
                    dve.wait_ge(lo_set, q * T + (t + 1))
                    nc.vector.tensor_tensor(sums_b[:, t], acc_b[:, t, :, 0:F1], sums_b[:, t], ALU.add
                                            ).then_inc(staged_b, 1)

            def compare(q, p, first):
                if p >= 4 or not first:
                    dve.wait_ge(mp_set, q * PAIRS + (p - 3))
                    dve.wait_ge(mn_set, q * PAIRS + (p - 3))
                for j in range(2):
                    k = 2 * p + j
                    m = mask[:, dsn(q % HALF, 1), k, :].rearrange("p s c -> p (s c)")
                    last = nc.vector.scalar_tensor_tensor(
                        vbuf[:, p % 4, j, :], f1b[:, dsn(of_turn(q) * GW, GW)], nf2[:, k:k + 1], m,
                        ALU.is_gt, ALU.add)
                last.then_inc(v_set, 1)

            def negative(q, p, first):
                dve.wait_ge(v_set, q * PAIRS + (p + 1))
                if p >= 2 or not first:
                    dve.wait_ge(m_used, q * PAIRS + (p - 1))
                nc.vector.tensor_scalar(mneg[:, p % 2], vbuf[:, p % 4], 2.0, None, ALU.is_equal
                                        ).then_inc(mn_set, 1)

            def turn(q, first=False, back=False):
                for p in range(PAIRS + 1):
                    if p == 0 and back:
                        dve.wait_ge(reloaded, q * 16 - 16 * (HALF - 1))
                    if first and p % 2 == 0 and p < PAIRS:
                        low_features(p // 2)
                    if first and p == 0:
                        dve.wait_ge(f1_in, 16)
                    if p < PAIRS:
                        compare(q, p, first)
                    if p == 2 and not first:
                        full_sums(q - 1)
                    if p == 6 and not first:
                        reciprocals_b(q - 1)
                    if p > 0:
                        negative(q, p - 1, first)

            turn(0, first=True)
            with dve.Fori(1, HALF) as q:
                turn(q)
            dve.wait_ge(f1_in, 32)
            with dve.Fori(HALF, GROUPS) as q:
                turn(q, back=True)
            full_sums(GROUPS - 1)
            reciprocals_b(GROUPS - 1)


_INS = ["x", "adj", "L0_gnn_h0", "L0_gnn_y", "L1_gnn_W", "L1_gnn_a1", "L1_gnn_a2"]


def kernel(**inputs):
    import numpy as _np
    import concourse.bacc as _bacc
    from concourse.bass_utils import run_bass_kernel_spmd as _run

    nc = _bacc.Bacc("TRN2", target_bir_lowering=False, num_devices=1)
    arrays, args = {}, []
    for name in _INS:
        a = _np.ascontiguousarray(inputs[name])
        arrays[f"in_{name}_dram"] = a
        args.append(nc.dram_tensor(f"in_{name}_dram", a.shape, mybir.dt.from_np(a.dtype),
                                   kind="ExternalInput").ap())
    out = nc.dram_tensor("out_0_dram", (N, F), F32, kind="ExternalOutput").ap()
    spill = nc.dram_tensor("mask_spill", (HALF, P, NT * GW), U8, kind="Internal").ap()
    f1_dram = nc.dram_tensor("f1_row", (NT, P), F32, kind="Internal").ap()
    graph_layers(nc, *args, out, spill, f1_dram)
    r = _run(nc, [arrays], core_ids=[0])
    return r.results[0]["out_0_dram"]
```

```python
from contextlib import ExitStack

import concourse.bass as bass
from concourse import mybir

ALU = mybir.AluOpType
ACT = mybir.ActivationFunctionType
F32 = mybir.dt.float32
F16 = mybir.dt.float16
BF16 = mybir.dt.bfloat16
U8 = mybir.dt.uint8
AX = mybir.AxisListType
RMAX = bass.bass_isa.ReduceOp.max

P = 128
N = 5000
F = 128
C = 16
GROUPS = 10
GR = N // GROUPS
T = 4
ST = (GR - P) // (T - 1)
DUP = P - ST
NT = GROUPS * T
GW = T * P
HALF = GROUPS // 2
SLOTS = 5
EPS = 1e-5
L1_EPS = 1e-12
H_SCALE = 1024.0
B_SCALE = 16384.0
SLOPE = 0.2
MIX = 0.9
PAIRS = NT // 2
FIRST = 2 * T
EARLY = NT - T
EARLY_PAIRS = 2
TAIL = (range(0, T - 1), range(T - 1, T))
NEG_ACT = (5, 9, 13)
F1 = F + 1
TW = 2 * F1 + 1
HT_STEPS, WH_STEPS = (26, 28), (30, 32)


def graph_layers(nc, x, adj, h0, y, w, a1, a2, out, spill, f1_dram):
    with ExitStack() as ctx:
        def sb(name, shape, dt=F32):
            return ctx.enter_context(nc.sbuf_tensor(name, shape, dt))

        def sem(name):
            return ctx.enter_context(nc.semaphore(name))

        mask = sb("mask", [P, HALF, NT, GW], U8)
        xs = sb("xs", [P, NT, F])
        stage = sb("stage", [P, T * 2 * F1])
        ident = sb("ident", [P, P])
        identb = sb("identb", [P, P], BF16)
        wx = sb("wx", [P, F + 2])
        mv = sb("mv", [P, NT, 2])
        inv = sb("inv", [P, NT])
        tmp = sb("tmp", [P, NT])
        stats1 = sb("stats1", [P, T, 6])
        mv1 = sb("mv1", [P, T, 2])
        const = sb("const", [P, 8])
        rec = sb("rec", [P, T])
        den = sb("den", [P, 2, T])
        arena = sb("arena", [P, 20790])

        def at(lo, n, dt=F32):
            v = arena[:, lo:lo + n]
            return v if dt == F32 else v.bitcast(dt)

        hm = at(0, NT * TW, F16).rearrange("p (k c) -> p k c", k=NT)
        wh = at(0, NT * TW).rearrange("p (k c) -> p k c", k=NT)[:, :, F1:TW]
        xm = hm[:, :, 0:4 * F1].rearrange("p k (m h c) -> p k m h c", m=2, h=2)
        yt = at(10360, 2560, F16)
        abuf = at(12920, 5000, BF16).rearrange("p (s t c) -> p s t c", s=SLOTS, t=T)
        gbuf = at(17920, 1024, F16).rearrange("p (s c) -> p s c", s=4)
        za = at(18944, 1024).rearrange("p (s t c) -> p s t c", s=2, t=T)
        zb = za[:, 0]
        hT = at(19968, 512)
        h0buf = za[:, 1]
        early = mask[:, HALF - 1].rearrange("p k c -> p (k c)")[:, 0:4 * 1000].bitcast(F32)
        ystage = early[:, 0:NT * C].rearrange("p (k c) -> p k c", k=NT)
        wraw, wT, araw = early[:, 640:768], early[:, 768:896], early[:, 896:898]
        stats = stage[:, 0:NT * 6].rearrange("p (k c) -> p k c", k=NT)
        f1b = at(10360, HALF * GW)
        vbuf = at(12920, 2048, BF16).rearrange("p (s j c) -> p s j c", s=4, j=2)
        mpos = at(14968, 2048, BF16).rearrange("p (s j c) -> p s j c", s=4, j=2)
        mneg = at(17016, 2048, BF16).rearrange("p (s j c) -> p s j c", s=4, j=2)
        raw = [v.rearrange("p (t h c) -> p t h c", t=T, h=2)
               for v in (stage[:, :], at(19064, T * 2 * F1))]
        hsb = at(19064, P)
        f1t = [at(12408 + P * i, P) for i in range(2)]
        bcol, dcol, bwc, dwc, sc, ac, cc = (at(20096 + NT * i, NT) for i in range(7))
        mw = at(20416, P)
        pm, gm, sm, hs1 = at(20550, 2), at(20554, 2), at(20558, 8), at(20568, 1)
        f12 = at(20620, 2 * NT)
        f1c, f2c = f12[:, 0:NT], f12[:, NT:2 * NT]
        hsum, top, nf2 = at(20700, 3 * GROUPS), at(20730, 2 * GROUPS), at(20750, NT)
        sums_a = stage[:, 0:T * (F + F1)].rearrange("p (t c) -> p t c", t=T)
        num = raw[0][:, :, 0, :]
        zs = stage[:, :].rearrange("p (t m c) -> p t m c", t=T, m=2)

        ps = ctx.enter_context(nc.psum_tensor("ps", [P, 8, 512], F32))
        bT = [ps[:, b, :].bitcast(BF16)[:, 0:GW] for b in (0, 1)]
        bP = ps[:, 1, :]
        bY = [ps[:, b, :] for b in (2, 3)]
        acc_a = ps[:, 4:8, 0:F + F1]
        acc_b = ps[:, :, 0:2 * F1].rearrange("p (t m) c -> p t m c", m=2)

        x_in = [sem(f"x_in{g}") for g in range(GROUPS)]
        y_in, w_in = sem("y_in"), sem("w_in")
        const_set, ident_set, identb_set = sem("const_set"), sem("ident_set"), sem("identb_set")
        dve_step, pool_step = sem("dve_step"), sem("pool_step")
        yt_raw, yt_set = sem("yt_raw"), sem("yt_set")
        wT_raw, wT_set, wa_raw, wx_set = sem("wT_raw"), sem("wT_set"), sem("wa_raw"), sem("wx_set")
        stats_set, var_set, std_set = sem("stats_set"), sem("var_set"), sem("std_set")
        za_set, za_split, h_set = sem("za_set"), sem("za_split"), sem("h_set")
        h0_in, h0_added = sem("h0_in"), sem("h0_added")
        adj_in = [sem(f"adj_in{i}") for i in range(SLOTS)]
        blk_t, blk_y = sem("blk_t"), sem("blk_y")
        mask_set, g_set = sem("mask_set"), sem("g_set")
        group_done, summed_a = sem("group_done"), sem("summed_a")
        staged_a, staged_v = sem("staged_a"), sem("staged_v")
        x1_set, spilled = sem("x1_set"), sem("spilled")
        var1_set, std1_set, zb_set = sem("var1_set"), sem("std1_set"), sem("zb_set")
        ht_raw, ht_set, wh_raw, wh_out = sem("ht_raw"), sem("ht_set"), sem("wh_raw"), sem("wh_out")
        hs_set, f1t_raw, f1t_set, f1_out, f1_in = (
            sem("hs_set"), sem("f1t_raw"), sem("f1t_set"), sem("f1_out"), sem("f1_in"))
        hsb_set, mean_raw, mw_set = sem("hsb_set"), sem("mean_raw"), sem("mw_set")
        pm_set, gm_set, sm_set, bd_set = sem("pm_set"), sem("gm_set"), sem("sm_set"), sem("bd_set")
        row_set, ac_set, bw_set = sem("row_set"), sem("ac_set"), sem("bw_set")
        zx_set, zx_hi, xm_set = sem("zx_set"), sem("zx_hi"), sem("xm_set")
        neg_step = sem("neg_step")
        reloaded, v_set = sem("reloaded"), sem("v_set")
        mp_set, mn_set, m_used = sem("mp_set"), sem("mn_set"), sem("m_used")
        tile_done, evac, fin = sem("tile_done"), sem("evac"), sem("fin")
        none_set, mean_in, rec_b = sem("none_set"), sem("mean_in"), sem("rec_b")
        relu_set, stage_free = sem("relu_set"), sem("stage_free")
        prep, top_set = sem("prep"), sem("top_set")
        out_ready, out_done = sem("out_ready"), sem("out_done")
        dve_turn, f12_set = sem("dve_turn"), sem("f12_set")

        def rows(src, row0, width, col0=0, ncols=None):
            v = src[bass.ds(row0, GR), :] if not isinstance(row0, int) else src[row0:row0 + GR, :]
            return bass.AP(tensor=v.tensor, offset=v.offset + col0,
                           ap=[[width, P], [ST * width, T], [1, ncols or width]])

        def of_turn(q):
            return (q + HALF) % GROUPS

        def dsn(i, n):
            return slice(i, i + n) if isinstance(i, int) else bass.ds(i, n)

        def one(v, i):
            return v[:, dsn(i, 1)].rearrange("p k c -> p (k c)")

        block = ctx.enter_context(nc.Block())

        @block.sync
        def _(sp):
            def load_f1(q):
                flat = f1_dram[of_turn(q) * T:(of_turn(q) + 1) * T, :]
                sp.dma_start(f1b[:, q % HALF * GW:(q % HALF + 1) * GW],
                             bass.AP(tensor=flat.tensor, offset=flat.offset, ap=[[0, P], [1, GW]])
                             ).then_inc(f1_in, 16)

            for g in range(GROUPS):
                sp.dma_start(xs[:, g * T:(g + 1) * T, :], rows(x, g * GR, F)).then_inc(x_in[g], 16)
            for g in range(GROUPS):
                if g:
                    sp.wait_ge(h0_added, g)
                else:
                    sp.wait_ge(h_set, GROUPS)
                sp.dma_start(h0buf, rows(h0, g * GR, F)).then_inc(h0_in, 16)
                if g < HALF:
                    sp.wait_ge(mask_set, (g + 1) * NT)
                    sp.dma_start(spill[g], mask[:, g].rearrange("p k c -> p (k c)")
                                 ).then_inc(spilled, 16)
                    sp.wait_ge(spilled, (g + 1) * 16)
            sp.wait_ge(f1t_set, 1)
            sp.dma_start(f1_dram[0:EARLY, :], f1t[0][0:EARLY, :]).then_inc(f1_out, 16)
            sp.wait_ge(f1_out, 16)
            for q in range(HALF - 1):
                if q:
                    sp.wait_ge(f1_in, q * 16)
                load_f1(q)
            sp.wait_ge(f1t_set, 2)
            sp.dma_start(f1_dram[EARLY:NT, :], f1t[1][0:NT - EARLY, :]).then_inc(f1_out, 16)
            sp.wait_ge(f1_out, 32)
            sp.wait_ge(f1_in, (HALF - 1) * 16)
            load_f1(HALF - 1)
            for q in range(GROUPS):
                if q < HALF:
                    sp.wait_ge(v_set, (q + 1) * PAIRS)
                    sp.dma_start(mask[:, q].rearrange("p k c -> p (k c)"), spill[q]).then_inc(reloaded, 16)
                    sp.wait_ge(f1_in, (q + HALF) * 16)
                    load_f1(q + HALF)
                    sp.wait_ge(reloaded, (q + 1) * 16)
                if q == HALF - 1:
                    done = range(HALF)
                elif q >= HALF:
                    done = (q,)
                else:
                    done = ()
                for d in done:
                    sp.wait_ge(out_ready, d + (len(TAIL) if d == GROUPS - 1 else 1))
                    g = (d + HALF) % GROUPS
                    o = out[g * GR:(g + 1) * GR, :]
                    sp.dma_start(bass.AP(tensor=o.tensor, offset=o.offset,
                                         ap=[[F, ST], [ST * F, T], [1, F]]),
                                 xs[0:ST, g * T:(g + 1) * T, :]).then_inc(out_done, 16)
                    sp.dma_start(out[g * GR + T * ST:(g + 1) * GR, :], xs[ST:P, g * T + T - 1, :]
                                 ).then_inc(out_done, 16)
            sp.wait_ge(out_done, 16 * 2 * GROUPS)

        @block.gpsimd
        def _(pool):
            nc.gpsimd.memset(ident[:], 0.0).then_inc(pool_step, 1)
            nc.gpsimd.memset(identb[:], 0.0).then_inc(pool_step, 1)
            nc.gpsimd.memset(const[:, 0:1], EPS).then_inc(const_set, 1)
            nc.gpsimd.memset(const[:, 1:2], -2.0).then_inc(const_set, 1)
            pool.wait_ge(pool_step, 2)
            for i, done in ((ident, ident_set), (identb, identb_set)):
                nc.gpsimd.affine_select(out=i[:], in_=i[:], compare_op=ALU.not_equal, fill=1.0,
                                        base=0, pattern=[[-1, P]], channel_multiplier=1).then_inc(done, 1)
            nc.gpsimd.memset(const[:, 3:4], 1.0).then_inc(const_set, 1)
            pool.wait_ge(x_in[4], 16)

            def load(g, i):
                pool.dma_start(abuf[:, i % SLOTS], rows(adj, g * GR, N, i * GR, GR)
                               ).then_inc(adj_in[i % SLOTS], 16)

            def add_parts(p):
                pool.wait_ge(staged_a, p + 1)
                pool.wait_ge(staged_v, p + 1)
                nc.gpsimd.tensor_tensor(sums_a[:, :, 0:F], sums_a[:, :, 0:F], sums_a[:, :, F1:F + F1],
                                        ALU.add).then_inc(summed_a, 1)

            def low_h(c):
                pool.wait_ge(za_split, 2 * c + 2)
                hg = hm[:, c * T:(c + 1) * T]
                nc.gpsimd.tensor_tensor(hg[:, :, F1:F + F1], za[:, c % 2], hg[:, :, 0:F], ALU.subtract
                                        ).then_inc(h_set, 1)

            for i in range(SLOTS):
                load(0, i)
            low_h(0)
            for i in range(GROUPS):
                if i + 1 < GROUPS:
                    low_h(i + 1)
                pool.wait_ge(blk_t, (i + 1) * T)
                load(0 if i + SLOTS < GROUPS else 1, (i + SLOTS) % GROUPS)
            add_parts(0)
            with pool.Fori(1, GROUPS - 1) as g:
                for i in range(GROUPS):
                    pool.wait_ge(blk_t, g * NT + (i + 1) * T)
                    load(g if i + SLOTS < GROUPS else g + 1, (i + SLOTS) % GROUPS)
                add_parts(g)
            for i in range(SLOTS):
                pool.wait_ge(blk_t, (GROUPS - 1) * NT + (i + 1) * T)
                load(GROUPS - 1, i + SLOTS)
            add_parts(GROUPS - 1)

            for i in range(2):
                pool.wait_ge(pm_set, i + 1)
                nc.gpsimd.partition_all_reduce(gm[:, i:i + 1], pm[:, i:i + 1], P, RMAX).then_inc(gm_set, 1)
            pool.wait_ge(bw_set, 1)
            for c in range(GROUPS):
                if c:
                    pool.wait_ge(xm_set, c)
                nc.gpsimd.tensor_tensor(
                    zs[:, :, 1, :], wh[:, c * T:(c + 1) * T, 0:F1],
                    dwc[:, c * T:(c + 1) * T].unsqueeze(2).to_broadcast([P, T, F1]), ALU.mult
                    ).then_inc(zx_set, 1)

        @block.tensor
        def _(pe):
            pe.wait_ge(ident_set, 1)
            pe.wait_ge(y_in, 16 * T)
            for g in range(GROUPS):
                if g >= 2:
                    pe.wait_ge(yt_set, g - 1)
                for t in range(T):
                    last = nc.tensor.transpose(ps[0:C, g % 2, t * P:(t + 1) * P],
                                               ystage[:, g * T + t, :], ident[:])
                last.then_inc(yt_raw, 1)
            pe.wait_ge(w_in, 48)
            nc.tensor.transpose(ps[:, 4, 0:F], wraw, ident[:]).then_inc(wT_raw, 1)
            pe.wait_ge(wT_set, 1)
            nc.tensor.matmul(ps[:, 5, 0:2], wT, araw, start=True, stop=True).then_inc(wa_raw, 1)

            def fill(g, k, lead=False):
                i = k // T
                if k % T == 0:
                    pe.wait_ge(adj_in[i % SLOTS], g * (16 * GROUPS // SLOTS) + 16 * (i // SLOTS + 1))
                if not lead:
                    pe.wait_ge(mask_set, g * NT + (k - 1))
                for t in range(T):
                    c = ST * (k % T)
                    last = nc.tensor.transpose(bT[k % 2][:, t * P:(t + 1) * P],
                                               abuf[:, i % SLOTS, t, c:c + P], identb[:])
                last.then_inc(blk_t, 1)

            def labels(g, k):
                nc.tensor.matmul(bY[k % 2], yt[0:C, k * P:(k + 1) * P], yt[0:C, dsn(g * GW, GW)],
                                 start=True, stop=True).then_inc(blk_y, 1)

            def add(g, k, first):
                if first and k % T == 0:
                    pe.wait_ge(h_set, k // T + 1)
                pe.wait_ge(g_set, g * NT + (k + 1))
                for t in range(T):
                    if k == 0 and not first and t % 2 == 0:
                        pe.wait_ge(staged_v if t else staged_a, g)
                    last = nc.tensor.matmul(acc_a[:, t, :], gbuf[:, k % 4, t * P:(t + 1) * P],
                                            hm[:, k, 0:F + F1], start=(k == 0), stop=(k == NT - 1))
                    if k == NT - 1 and t % 2:
                        last.then_inc(group_done, 1)

            def transpose_h(p, part, bank=bP):
                pe.wait_ge(zb_set, p + 1)
                for t in (2 * part, 2 * part + 1):
                    last = nc.tensor.transpose(bank[:, t * P:(t + 1) * P], zb[:, t, :], ident[:])
                last.then_inc(ht_raw, 1)

            def project(p, part, bank=bP):
                pe.wait_ge(ht_set, p * 2 + (part + 1))
                for i in range(2):
                    t = 2 * part + i
                    last = nc.tensor.matmul(bank[:, i * (F + 2):(i + 1) * (F + 2)], hT[:, t * P:(t + 1) * P],
                                            wx[:], start=True, stop=True)
                last.then_inc(wh_raw, 1)

            def group_a(g, first=False, final=False):
                for k in range(NT):
                    ahead = (g if k + 2 < NT else g + 1, (k + 2) % NT)
                    going = not (final and k + 2 >= NT)
                    if not first:
                        if k - 1 in HT_STEPS:
                            pe.wait_ge(ht_set, g * 2 + (HT_STEPS.index(k - 1) - 1))
                        if k - 1 in WH_STEPS:
                            pe.wait_ge(wh_out, g * 2 + (WH_STEPS.index(k - 1) - 1))
                    if going:
                        fill(*ahead)
                    if not first and k in (*HT_STEPS, *WH_STEPS):
                        pe.wait_ge(mask_set, g * NT + (k + 2))
                        if k in HT_STEPS:
                            transpose_h(g - 1, HT_STEPS.index(k))
                        else:
                            project(g - 1, WH_STEPS.index(k))
                    if k == 0 and not first:
                        pe.wait_ge(g_set, g * NT + (k + 1))
                        labels(*ahead)
                    add(g, k, first)
                    if going and (k or first):
                        labels(*ahead)

            pe.wait_ge(identb_set, 1)
            pe.wait_ge(yt_set, GROUPS)
            for k in range(2):
                fill(0, k, True)
                labels(0, k)
            group_a(0, first=True)
            with pe.Fori(1, GROUPS - 1) as g:
                group_a(g)
            group_a(GROUPS - 1, final=True)

            pe.wait_ge(f12_set, 1)
            nc.tensor.transpose(ps[0:EARLY, 2, 0:P], f12[:, 0:EARLY], ident[:]).then_inc(f1t_raw, 1)
            pe.wait_ge(mask_set, GROUPS * NT)
            transpose_h(GROUPS - 1, 0)
            transpose_h(GROUPS - 1, 1, ps[:, 0, :])
            pe.wait_ge(f1t_set, 1)
            for part in range(2):
                project(GROUPS - 1, part, bY[part])
            pe.wait_ge(f12_set, 2)
            nc.tensor.transpose(ps[0:NT - EARLY, 0, 0:P], f1c[:, EARLY:NT], ident[:]).then_inc(f1t_raw, 1)
            pe.wait_ge(f1t_set, 2)
            pe.wait_ge(staged_a, GROUPS)
            pe.wait_ge(staged_v, GROUPS)

            def mean_wh():
                pe.wait_ge(hsb_set, 1)
                nc.tensor.matmul(ps[:, 2, 0:F], hsb, wx[:, 0:F], start=True, stop=True).then_inc(mean_raw, 1)
                pe.wait_ge(mw_set, 1)

            mean_wh()

            def turn(q, first=False):
                for p in range(PAIRS):
                    if first and p % 2 == 0:
                        pe.wait_ge(xm_set, p // 2 + 1)
                    pe.wait_ge(mp_set, q * PAIRS + (p + 1))
                    pe.wait_ge(mn_set, q * PAIRS + (p + 1))
                    for t in range(T):
                        if p == 0 and not first:
                            pe.wait_ge(evac, q * T + (t + 1 - T))
                        for j in range(2):
                            k = 2 * p + j
                            for m, src in enumerate((mpos, mneg)):
                                last = nc.tensor.matmul(
                                    acc_b[:, t, m, :], src[:, p % 4, j, t * P:(t + 1) * P],
                                    xm[:, k, m].rearrange("p h c -> p (h c)"),
                                    start=(k == 0), stop=(k == NT - 1))
                        if p == PAIRS - 1:
                            last.then_inc(tile_done, 1)
                    if p < PAIRS - 1:
                        last.then_inc(m_used, 1)
                    else:
                        pe.wait_ge(tile_done, q * T + T)
                        pe.sem_inc(m_used, 1)

            turn(0, first=True)
            with pe.Fori(1, GROUPS) as q:
                turn(q)

        @block.scalar
        def _(act):
            for t in range(T):
                act.dma_start(ystage.rearrange("p (g t) c -> p g t c", t=T)[:, :, t, :],
                              bass.AP(tensor=y.tensor, offset=y.offset + t * ST * C,
                                      ap=[[C, P], [GR * C, GROUPS], [1, C]])).then_inc(y_in, 16)
            act.dma_start(wraw, w).then_inc(w_in, 16)
            act.dma_start(araw[:, 0:1], a1).then_inc(w_in, 16)
            act.dma_start(araw[:, 1:2], a2).then_inc(w_in, 16)

            def deviation_0(i, lo, hi):
                act.wait_ge(var_set, i + 1)
                nc.scalar.activation(inv[:, lo:hi], mv[:, lo:hi, 1], ACT.Sqrt, bias=const[:, 0:1]
                                     ).then_inc(std_set, 1)

            act.wait_ge(const_set, 3)
            deviation_0(0, 0, FIRST)
            for g in range(GROUPS):
                act.wait_ge(yt_raw, g + 1)
                nc.scalar.copy(yt[0:C, g * GW:(g + 1) * GW], ps[0:C, g % 2, :]).then_inc(yt_set, 1)
            act.wait_ge(wT_raw, 1)
            nc.scalar.copy(wT, ps[:, 4, 0:F]).then_inc(wT_set, 1)
            act.wait_ge(wa_raw, 1)
            nc.scalar.copy(wx[:, F:F + 2], ps[:, 5, 0:2]).then_inc(wx_set, 1)
            nc.scalar.copy(wx[:, 0:F], wraw).then_inc(wx_set, 1)

            def high_h(c):
                act.wait_ge(za_set, c + 1)
                nc.scalar.activation(hm[:, c * T:(c + 1) * T, 0:F], za[:, c % 2], ACT.Relu, scale=H_SCALE
                                     ).then_inc(za_split, 1)

            def full_h(c):
                nc.scalar.activation(za[:, c % 2], za[:, c % 2], ACT.Relu, scale=H_SCALE
                                     ).then_inc(za_split, 1)

            def stage_a(p):
                act.wait_ge(group_done, p * 2 + 1)
                nc.scalar.copy(sums_a[:, 0:2, :], acc_a[:, 0:2, :]).then_inc(staged_a, 1)

            def deviation(p):
                act.wait_ge(var1_set, p + 1)
                nc.scalar.activation(inv[:, dsn(p * T, T)], mv[:, dsn(p * T, T), 1], ACT.Sqrt,
                                     bias=const[:, 0:1]).then_inc(std1_set, 1)

            def relu_h(p, part, bank=bP):
                act.wait_ge(ht_raw, p * 2 + (part + 1))
                c = slice(2 * part * P, 2 * (part + 1) * P)
                nc.scalar.activation(hT[:, c], bank[:, c], ACT.Relu).then_inc(ht_set, 1)

            def collect(p, part, bank=bP):
                act.wait_ge(wh_raw, p * 2 + (part + 1))
                nc.scalar.copy(wh[:, dsn(p * T + 2 * part, 2), :],
                               bank[:, 0:2 * (F + 2)].rearrange("p (t c) -> p t c", t=2)
                               ).then_inc(wh_out, 1)

            def group_a(g, first=False, over=False):
                for k in range(NT):
                    if k == 0 and over:
                        act.wait_ge(spilled, g * 16 - 16 * (HALF - 1))
                    if not first and k - 2 in HT_STEPS:
                        relu_h(g - 1, HT_STEPS.index(k - 2))
                    act.wait_ge(blk_t, g * NT + (k + 1))
                    nc.scalar.activation(mask[:, dsn(g % HALF, 1), k, :].rearrange("p s c -> p (s c)"),
                                         bT[k % 2], ACT.Copy, scale=2.0).then_inc(mask_set, 1)
                    if first and k % T < 2 and k // T + 1 < GROUPS:
                        (high_h, full_h)[k % T](k // T + 1)
                    if not first:
                        if k == 1:
                            stage_a(g - 1)
                        if k == 15:
                            deviation(g - 1)
                        if k - 2 in WH_STEPS:
                            collect(g - 1, WH_STEPS.index(k - 2))

            high_h(0)
            full_h(0)
            deviation_0(1, FIRST, NT)
            group_a(0, first=True)
            with act.Fori(1, HALF) as g:
                group_a(g)
            with act.Fori(HALF, GROUPS) as g:
                group_a(g, over=True)
            stage_a(GROUPS - 1)
            act.wait_ge(f1t_raw, 1)
            nc.scalar.copy(f1t[0][0:EARLY, :], ps[0:EARLY, 2, 0:P]).then_inc(f1t_set, 1)
            deviation(GROUPS - 1)
            nc.scalar.activation(const[:, 2:3], const[:, 0:1], ACT.Exp)
            for part, bank in enumerate((bP, ps[:, 0, :])):
                relu_h(GROUPS - 1, part, bank)
            for part in range(2):
                collect(GROUPS - 1, part, bY[part])

            def hi_features(c):
                if c:
                    act.wait_ge(xm_set, c)
                for t in range(T):
                    k = c * T + t
                    last = nc.scalar.activation(zs[:, t, 0, :], wh[:, k, 0:F1], ACT.Copy,
                                                scale=bwc[:, k:k + 1])
                last.then_inc(zx_set, 1)
                act.wait_ge(zx_set, 2 * c + 2)
                nc.scalar.copy(xm[:, c * T:(c + 1) * T, :, 0, :], zs).then_inc(zx_hi, 1)

            def positive(q, p, first):
                act.wait_ge(v_set, q * PAIRS + (p + 1))
                if p >= 4 or not first:
                    act.wait_ge(m_used, q * PAIRS + (p - 3))
                if p in NEG_ACT and not first:
                    done = 2 * (NEG_ACT.index(p) - len(NEG_ACT))
                    per = 2 * len(NEG_ACT)
                    nc.scalar.activation(mneg[:, p % 4], vbuf[:, p % 4], ACT.Abs, bias=const[:, 1:2]
                                         ).then_inc(neg_step, 1)
                    act.wait_ge(neg_step, q * per + (done + 1))
                    nc.scalar.activation(mneg[:, p % 4], mneg[:, p % 4], ACT.Relu, bias=const[:, 3:4],
                                         scale=-1.0).then_inc(neg_step, 1)
                    act.wait_ge(neg_step, q * per + (done + 2))
                nc.scalar.activation(mpos[:, p % 4], vbuf[:, p % 4], ACT.Relu, bias=const[:, 1:2]
                                     ).then_inc(mp_set, 1)

            def evacuate(q):
                act.wait_ge(stage_free, q + 1)
                g4 = of_turn(q) * T
                for t in range(T):
                    act.wait_ge(tile_done, q * T + (t + 1))
                    for m, factor in enumerate((ac, cc)):
                        last = nc.scalar.activation(raw[m][:, t].rearrange("p h c -> p (h c)"),
                                                    acc_b[:, t, m, :], ACT.Copy,
                                                    scale=factor[:, dsn(g4 + t, 1)])
                    last.then_inc(evac, 1)

            def edgeless(q, part=0, tiles=range(T)):
                act.wait_ge(none_set, q + 1 + part)
                for t in tiles:
                    last = nc.scalar.activation(raw[1][:, t, 0, 0:F], mw, ACT.Copy,
                                                scale=den[:, 0, t:t + 1])
                last.then_inc(mean_in, 1)

            def divide(q, part=0, tiles=range(T)):
                act.wait_ge(rec_b, q + 1 + part)
                for t in tiles:
                    last = nc.scalar.activation(num[:, t, 0:F], num[:, t, 0:F], ACT.Relu,
                                                scale=rec[:, t:t + 1])
                last.then_inc(relu_set, 1)

            def turn(q, first=False):
                for p in range(PAIRS):
                    if p >= EARLY_PAIRS or not first:
                        positive(q, p, first)
                    if not first:
                        if p == 1:
                            act.wait_ge(ac_set, 2)
                            evacuate(q - 1)
                        if p == 9:
                            act.wait_ge(mw_set, 1)
                            edgeless(q - 1)
                        if p == 14:
                            divide(q - 1)
                    if first and p % 2 == 0 and p // 2 + 1 < GROUPS:
                        hi_features(p // 2 + 1)
                    if first and p == 1:
                        act.wait_ge(row_set, 2)
                        nc.scalar.activation(ac, ac, ACT.Exp).then_inc(ac_set, 1)
                        nc.scalar.activation(cc, cc, ACT.Exp).then_inc(ac_set, 1)

            positive(0, 0, True)
            act.wait_ge(sm_set, 2)
            nc.scalar.activation(bcol, f2c, ACT.Exp, bias=sm[:, 0:1]).then_inc(bd_set, 1)
            nc.scalar.activation(dcol, f2c, ACT.Exp, bias=sm[:, 1:2], scale=SLOPE).then_inc(bd_set, 1)
            act.wait_ge(f1t_raw, 2)
            nc.scalar.copy(f1t[1][0:NT - EARLY, :], ps[0:NT - EARLY, 0, 0:P]).then_inc(f1t_set, 1)
            for p in range(1, EARLY_PAIRS):
                positive(0, p, True)
            act.wait_ge(bw_set, 1)
            hi_features(0)
            turn(0, first=True)
            with act.Fori(1, GROUPS) as q:
                turn(q)
            evacuate(GROUPS - 1)
            for i, tiles in enumerate(TAIL):
                edgeless(GROUPS - 1, i, tiles)
                divide(GROUPS - 1, i, tiles)

        @block.vector
        def _(dve):
            step = [0]

            def chain(ins):
                step[0] += 1
                ins.then_inc(dve_step, 1)
                dve.wait_ge(dve_step, step[0])

            chain(nc.vector.memset(hm[:, :, F:F1], 1.0))
            nc.vector.memset(hm[0:DUP].rearrange("p (g t) c -> p g t c", t=T)[:, :, 1:T, F], 0.0)

            def statistics(g):
                if g < GROUPS:
                    dve.wait_ge(x_in[g], 16)
                    for k in range(g * T, g * T + T):
                        last = nc.vector.bn_stats(stats[:, k, :], xs[:, k, :])
                    last.then_inc(stats_set, 1)

            def aggregate(g):
                dve.wait_ge(stats_set, g + 1)
                for k in range(g * T, g * T + T):
                    last = nc.vector.bn_aggr(mv[:, k, :], stats[:, k, :])
                if g in (FIRST // T - 1, GROUPS - 1):
                    last.then_inc(var_set, 1)

            def newton(lo, n):
                i, t, v = inv[:, lo:lo + n], tmp[:, 0:n], mv[:, lo:lo + n, 1]
                chain(nc.vector.reciprocal(t, i))
                chain(nc.vector.scalar_tensor_tensor(t, v, EPS, t, ALU.add, ALU.mult))
                chain(nc.vector.tensor_tensor(t, t, i, ALU.add))
                chain(nc.vector.tensor_scalar(t, t, 0.5, None, ALU.mult))
                chain(nc.vector.reciprocal(i, t))
                chain(nc.vector.memset(i[0:DUP].rearrange("p (g t) -> p g t", t=T)[:, :, 1:T], 0.0))

            def normalise(dst, g, tiles=range(T)):
                for t in tiles:
                    k = g * T + t
                    last = nc.vector.tensor_scalar(dst[:, t, :], one(xs, k), mv[:, dsn(k, 1), 0],
                                                   inv[:, dsn(k, 1)], ALU.subtract, ALU.mult)
                return last

            def rows_0(c, tiles=range(T)):
                if c >= 2 and 0 in tiles:
                    dve.wait_ge(h_set, c - 1)
                last = normalise(za[:, c % 2], c, tiles)
                if T - 1 in tiles:
                    last.then_inc(za_set, 1)

            def stage_v(p):
                dve.wait_ge(group_done, p * 2 + 2)
                nc.vector.tensor_copy(sums_a[:, 2:4, :], acc_a[:, 2:4, :]).then_inc(staged_v, 1)

            def recip(p):
                dve.wait_ge(staged_a, p + 1)
                dve.wait_ge(staged_v, p + 1)
                nc.vector.tensor_scalar(rec[:], sums_a[:, :, F], L1_EPS, H_SCALE / MIX, ALU.max, ALU.mult
                                        ).then_inc(prep, 1)

            def recip2(p):
                dve.wait_ge(prep, p * PREP + 1)
                nc.vector.reciprocal(rec[:], rec[:]).then_inc(prep, 1)

            def add_h0(p, half):
                dve.wait_ge(h0_in, p * 16 + 16)
                xg = xs[:, dsn(p * T + 2 * half, 2), :].rearrange("p t c -> p (t c)")
                last = nc.vector.scalar_tensor_tensor(
                    xg, h0buf[:, 2 * half:2 * half + 2].rearrange("p t c -> p (t c)"), 1.0 - MIX, xg,
                    ALU.mult, ALU.add)
                if half:
                    last.then_inc(h0_added, 1)

            def update(p, t):
                if t == 0:
                    dve.wait_ge(h0_added, p + 1)
                    dve.wait_ge(prep, p * PREP + 2)
                    dve.wait_ge(summed_a, p + 1)
                xk = one(xs, p * T + t)
                nc.vector.scalar_tensor_tensor(xk, sums_a[:, t, 0:F], rec[:, t:t + 1], xk,
                                               ALU.mult, ALU.add).then_inc(x1_set, 1)

            def moments(p, t):
                dve.wait_ge(x1_set, p * T + (t + 1))
                dve.sem_inc(dve_turn, 1)
                nc.vector.bn_stats(stats1[:, t, :], one(xs, p * T + t)).then_inc(prep, 1)

            def gather(p):
                dve.wait_ge(prep, p * PREP + 6)
                dve.sem_inc(dve_turn, 1)
                for t in range(T):
                    last = nc.vector.bn_aggr(mv1[:, t, :], stats1[:, t, :])
                last.then_inc(prep, 1)

            def keep(p):
                dve.wait_ge(prep, p * PREP + 7)
                nc.vector.tensor_copy(mv[:, dsn(p * T, T), :], mv1[:, :, :]).then_inc(var1_set, 1)

            def newton_step(p, i):
                if i == 0:
                    dve.wait_ge(std1_set, p + 1)
                else:
                    dve.wait_ge(prep, p * PREP + (7 + i))
                dve.sem_inc(dve_turn, 1)
                for n, make in enumerate(NEWTON):
                    if n == i:
                        make(inv[:, dsn(p * T, T)], tmp[:, 0:T], mv[:, dsn(p * T, T), 1]).then_inc(prep, 1)

            NEWTON = (
                lambda i, t, v: nc.vector.reciprocal(t, i),
                lambda i, t, v: nc.vector.scalar_tensor_tensor(t, v, EPS, t, ALU.add, ALU.mult),
                lambda i, t, v: nc.vector.tensor_tensor(t, t, i, ALU.add),
                lambda i, t, v: nc.vector.tensor_scalar(t, t, 0.5, None, ALU.mult),
                lambda i, t, v: nc.vector.reciprocal(i, t),
            )
            PREP = 12

            def rows_h(p, t):
                if t == 0:
                    dve.wait_ge(prep, p * PREP + PREP)
                last = normalise(zb, p, (t,))
                if t == T - 1:
                    last.then_inc(zb_set, 1)

            def sum_h(p, part):
                dve.wait_ge(ht_set, p * 2 + (part + 1))
                hv = hT.rearrange("p (t c) -> p t c", t=T)
                last = nc.vector.tensor_reduce(hsum[:, dsn(p * 3 + part, 1)],
                                               hv[:, 2 * part:2 * part + 2, DUP:P], AX.XY, ALU.add)
                if part:
                    last = nc.vector.tensor_reduce(hsum[:, dsn(p * 3 + 2, 1)], hv[:, 0, 0:DUP], AX.X,
                                                   ALU.add)
                last.then_inc(hs_set, 1)

            def largest(p, part):
                dve.wait_ge(wh_out, p * 2 + (part + 1))
                nc.vector.tensor_reduce(top[:, dsn(p * 2 + part, 1)], wh[:, dsn(p * T + 2 * part, 2), 0:F],
                                        AX.XY, ALU.max, apply_absolute_value=True).then_inc(top_set, 1)

            PARTS = {
                0: lambda p: stage_v(p), 1: lambda p: add_h0(p, 0), 2: lambda p: add_h0(p, 1),
                3: lambda p: recip(p), 4: lambda p: recip2(p),
                5: lambda p: update(p, 0), 6: lambda p: update(p, 1),
                7: lambda p: update(p, 2), 8: lambda p: update(p, 3),
                9: lambda p: moments(p, 0), 10: lambda p: moments(p, 1),
                11: lambda p: moments(p, 2), 12: lambda p: moments(p, 3),
                13: lambda p: gather(p), 14: lambda p: keep(p),
                17: lambda p: newton_step(p, 0), 18: lambda p: newton_step(p, 1),
                19: lambda p: newton_step(p, 2), 20: lambda p: newton_step(p, 3),
                21: lambda p: newton_step(p, 4), 22: lambda p: rows_h(p, 0), 23: lambda p: rows_h(p, 1),
                24: lambda p: rows_h(p, 2), 25: lambda p: rows_h(p, 3),
                HT_STEPS[0] + 3: lambda p: sum_h(p, 0), HT_STEPS[1] + 3: lambda p: sum_h(p, 1),
                WH_STEPS[0] + 3: lambda p: largest(p, 0), WH_STEPS[1] + 3: lambda p: largest(p, 1),
            }

            def group_a(g, first=False):
                for k in range(NT):
                    dve.wait_ge(mask_set, g * NT + (k + 1))
                    dve.wait_ge(blk_y, g * NT + (k + 1))
                    m = mask[:, dsn(g % HALF, 1), k, :].rearrange("p s c -> p (s c)")
                    nc.vector.scalar_tensor_tensor(gbuf[:, k % 4, :], m, 0.5, bY[k % 2],
                                                   ALU.mult, ALU.mult).then_inc(g_set, 1)
                    if first and k // T + 2 < GROUPS:
                        rows_0(k // T + 2, (k % T,))
                    if not first and k in PARTS:
                        PARTS[k](g - 1)

            for g in range(FIRST // T + 1):
                statistics(g)
                if g:
                    aggregate(g - 1)
            for g in range(FIRST // T + 1, FIRST // T + 3):
                statistics(g)
                aggregate(g - 1)
            dve.wait_ge(std_set, 1)
            newton(0, FIRST)
            rows_0(0)
            rows_0(1)
            for g in range(FIRST // T + 3, GROUPS + 1):
                statistics(g)
                aggregate(g - 1)
            dve.wait_ge(std_set, 2)
            newton(FIRST, NT - FIRST)
            group_a(0, first=True)
            with dve.Fori(1, GROUPS) as g:
                group_a(g)

            def compare(q, p, first):
                if p >= 4 or not first:
                    dve.wait_ge(mp_set, q * PAIRS + (p - 3))
                    dve.wait_ge(mn_set, q * PAIRS + (p - 3))
                for j in range(2):
                    k = 2 * p + j
                    m = mask[:, dsn(q % HALF, 1), k, :].rearrange("p s c -> p (s c)")
                    last = nc.vector.scalar_tensor_tensor(
                        vbuf[:, p % 4, j, :], f1b[:, dsn(q % HALF * GW, GW)], nf2[:, k:k + 1], m,
                        ALU.is_gt, ALU.add)
                last.then_inc(v_set, 1)

            def negative(q, p, first):
                dve.wait_ge(v_set, q * PAIRS + (p + 1))
                if p in NEG_ACT and not first:
                    dve.wait_ge(mn_set, q * PAIRS + p)
                    dve.sem_inc(mn_set, 1)
                    return
                if p >= 4 or not first:
                    dve.wait_ge(m_used, q * PAIRS + (p - 3))
                nc.vector.tensor_scalar(mneg[:, p % 4], vbuf[:, p % 4], 2.0, None, ALU.is_equal
                                        ).then_inc(mn_set, 1)

            def columns(lo, hi):
                nc.vector.tensor_copy(f12.rearrange("p (c k) -> p c k", c=2)[:, :, lo:hi],
                                      wh[:, lo:hi, F:F + 2].rearrange("p k c -> p c k")
                                      ).then_inc(f12_set, 1)
                chain(nc.vector.tensor_scalar(nf2[:, lo:hi], wh[:, lo:hi, F + 1], -1.0, None, ALU.mult))

            columns(0, EARLY)
            for k in sorted(PARTS):
                if k <= HT_STEPS[0]:
                    PARTS[k](GROUPS - 1)
            dve.wait_ge(f1_in, 16)
            for p in range(EARLY_PAIRS):
                compare(0, p, True)
                negative(0, p, True)
            for part in range(2):
                sum_h(GROUPS - 1, part)
            largest(GROUPS - 1, 0)
            dve.wait_ge(wh_out, 2 * GROUPS)
            columns(EARLY, NT)
            dve.wait_ge(f12_set, 2)
            nc.vector.tensor_reduce(pm[:, 0:1], f2c, AX.X, ALU.max).then_inc(pm_set, 1)
            largest(GROUPS - 1, 1)
            dve.wait_ge(top_set, 2 * GROUPS)
            nc.vector.tensor_reduce(pm[:, 1:2], top, AX.X, ALU.max).then_inc(pm_set, 1)
            dve.wait_ge(gm_set, 1)
            nc.vector.tensor_scalar(sm[:, 0:1], gm[:, 0:1], -1.0, None, ALU.mult).then_inc(sm_set, 1)
            nc.vector.tensor_scalar(sm[:, 1:2], gm[:, 0:1], -SLOPE, None, ALU.mult).then_inc(sm_set, 1)
            dve.wait_ge(gm_set, 2)
            chain(nc.vector.tensor_scalar(sm[:, 2:3], gm[:, 1:2], 1e-30, None, ALU.max))
            chain(nc.vector.reciprocal(sm[:, 3:4], sm[:, 2:3]))
            nc.vector.tensor_scalar(wh[:, :, F], f2c, 0.0, sm[:, 2:3], ALU.mult, ALU.add)
            chain(nc.vector.tensor_scalar(sc, f1c, gm[:, 0:1], None, ALU.add))
            nc.vector.tensor_scalar(ac, sc, 1.0 - SLOPE, 0.0, ALU.mult, ALU.min).then_inc(row_set, 1)
            nc.vector.tensor_scalar(cc, sc, SLOPE - 1.0, 0.0, ALU.mult, ALU.min).then_inc(row_set, 1)
            dve.wait_ge(bd_set, 2)
            for colv in (bcol, dcol):
                chain(nc.vector.memset(colv.rearrange("p (g t) -> p g t", t=T)[0:DUP, :, 1:T], 0.0))
            nc.vector.tensor_scalar(bwc, bcol, sm[:, 3:4], B_SCALE, ALU.mult, ALU.mult)
            nc.vector.tensor_scalar(dwc, dcol, sm[:, 3:4], B_SCALE, ALU.mult, ALU.mult).then_inc(bw_set, 1)
            dve.wait_ge(hs_set, 2 * GROUPS)
            chain(nc.vector.tensor_reduce(hs1, hsum, AX.X, ALU.add))
            chain(nc.vector.tensor_scalar(hs1, hs1, 1.0 / N, None, ALU.mult))
            nc.vector.tensor_scalar(hsb, ident[:], 0.0, hs1, ALU.mult, ALU.add).then_inc(hsb_set, 1)
            dve.wait_ge(mean_raw, 1)
            nc.vector.tensor_scalar(mw, ps[:, 2, 0:F], sm[:, 3:4], None, ALU.mult).then_inc(mw_set, 1)

            def low_features(c):
                dve.wait_ge(zx_hi, c + 1)
                xg = xm[:, c * T:(c + 1) * T]
                nc.vector.tensor_tensor(xg[:, :, :, 1, :], zs, xg[:, :, :, 0, :], ALU.subtract
                                        ).then_inc(xm_set, 1)

            FIN = 5

            def add_sums(q):
                dve.wait_ge(evac, q * T + T)
                nc.vector.tensor_tensor(raw[0], raw[0], raw[1], ALU.add).then_inc(fin, 1)

            def add_low(q):
                dve.wait_ge(fin, q * FIN + 1)
                nc.vector.tensor_tensor(num, num, raw[0][:, :, 1, :], ALU.add).then_inc(fin, 1)

            def edgeless(q):
                dve.wait_ge(fin, q * FIN + 2)
                nc.vector.tensor_scalar(den[:, 0, :], num[:, :, F], 0.0, None, ALU.is_equal
                                        ).then_inc(none_set, 1)

            def whole(q):
                dve.wait_ge(none_set, q + 1)
                nc.vector.tensor_tensor(den[:, 1, :], num[:, :, F], den[:, 0, :], ALU.add
                                        ).then_inc(fin, 1)

            def invert(q):
                dve.wait_ge(fin, q * FIN + 3)
                nc.vector.reciprocal(den[:, 1, :], den[:, 1, :]).then_inc(fin, 1)

            def scale_rec(q):
                dve.wait_ge(fin, q * FIN + 4)
                nc.vector.tensor_scalar(rec[:], den[:, 1, :], sm[:, 2:3], None, ALU.mult).then_inc(fin, 1)

            def add_mean(q):
                dve.wait_ge(mean_in, q + 1)
                dve.wait_ge(fin, q * FIN + 5)
                nc.vector.tensor_tensor(num[:, :, 0:F], num[:, :, 0:F], raw[1][:, :, 0, 0:F], ALU.add
                                        ).then_inc(rec_b, 1)

            def result(q):
                dve.wait_ge(relu_set, q + 1)
                xg = xs[:, dsn(of_turn(q) * T, T), :]
                nc.vector.tensor_tensor(xg, xg, num[:, :, 0:F], ALU.add).then_inc(out_ready, 1)

            def free_stage(q):
                dve.wait_ge(out_ready, q + 1)
                dve.sem_inc(stage_free, 1)

            RESULT = {
                5: lambda q: add_sums(q), 6: lambda q: add_low(q), 7: lambda q: edgeless(q),
                8: lambda q: whole(q), 9: lambda q: invert(q), 10: lambda q: scale_rec(q),
                14: lambda q: add_mean(q), 18: lambda q: result(q), 19: lambda q: free_stage(q),
            }

            def turn(q, first=False, back=False):
                for p in range(PAIRS + 1):
                    if p == 0 and back:
                        dve.wait_ge(reloaded, q * 16 - 16 * (HALF - 1))
                    if p == 0 and not first:
                        dve.wait_ge(f1_in, q * 16 + 16)
                    early = first and p < EARLY_PAIRS
                    if p < PAIRS and not early:
                        compare(q, p, first)
                    if first and p % 2 == 0 and p < PAIRS:
                        low_features(p // 2)
                    if not first and p in RESULT:
                        RESULT[p](q - 1)
                    if p > 0 and not (first and p - 1 < EARLY_PAIRS):
                        negative(q, p - 1, first)

            turn(0, first=True)
            dve.wait_ge(xm_set, GROUPS)
            dve.sem_inc(stage_free, 1)
            with dve.Fori(1, HALF) as q:
                turn(q)
            with dve.Fori(HALF, GROUPS) as q:
                turn(q, back=True)
            for i, tiles in enumerate(TAIL):
                ts = slice(tiles[0], tiles[-1] + 1)
                dve.wait_ge(evac, (GROUPS - 1) * T + ts.stop)
                chain(nc.vector.tensor_tensor(raw[0][:, ts], raw[0][:, ts], raw[1][:, ts], ALU.add))
                chain(nc.vector.tensor_tensor(num[:, ts], num[:, ts], raw[0][:, ts, 1, :], ALU.add))
                nc.vector.tensor_scalar(den[:, 0, ts], num[:, ts, F], 0.0, None, ALU.is_equal
                                        ).then_inc(none_set, 1)
                dve.wait_ge(none_set, GROUPS + i)
                chain(nc.vector.tensor_tensor(den[:, 1, ts], num[:, ts, F], den[:, 0, ts], ALU.add))
                chain(nc.vector.reciprocal(den[:, 1, ts], den[:, 1, ts]))
                chain(nc.vector.tensor_scalar(rec[:, ts], den[:, 1, ts], sm[:, 2:3], None, ALU.mult))
                dve.wait_ge(mean_in, GROUPS + i)
                nc.vector.tensor_tensor(num[:, ts, 0:F], num[:, ts, 0:F], raw[1][:, ts, 0, 0:F], ALU.add
                                        ).then_inc(rec_b, 1)
            for i, tiles in enumerate(TAIL):
                ts = slice(tiles[0], tiles[-1] + 1)
                k = of_turn(GROUPS - 1) * T
                dve.wait_ge(relu_set, GROUPS + i)
                xg = xs[:, k + ts.start:k + ts.stop, :]
                nc.vector.tensor_tensor(xg, xg, num[:, ts, 0:F], ALU.add).then_inc(out_ready, 1)


_INS = ["x", "adj", "L0_gnn_h0", "L0_gnn_y", "L1_gnn_W", "L1_gnn_a1", "L1_gnn_a2"]


def kernel(**inputs):
    import numpy as _np
    import concourse.bacc as _bacc
    from concourse.bass_utils import run_bass_kernel_spmd as _run

    nc = _bacc.Bacc("TRN2", target_bir_lowering=False, num_devices=1)
    arrays, args = {}, []
    for name in _INS:
        a = _np.ascontiguousarray(inputs[name])
        arrays[f"in_{name}_dram"] = a
        args.append(nc.dram_tensor(f"in_{name}_dram", a.shape, mybir.dt.from_np(a.dtype),
                                   kind="ExternalInput").ap())
    out = nc.dram_tensor("out_0_dram", (N, F), F32, kind="ExternalOutput").ap()
    spill = nc.dram_tensor("mask_spill", (HALF, P, NT * GW), U8, kind="Internal").ap()
    f1_dram = nc.dram_tensor("f1_row", (NT, P), F32, kind="Internal").ap()
    graph_layers(nc, *args, out, spill, f1_dram)
    r = _run(nc, [arrays], core_ids=[0])
    return r.results[0]["out_0_dram"]
```
